# Optimizing a Trainium2 kernel written in Bass

```python
import numpy as np
import jax
import jax.numpy as jnp

def _softmax(x, axis=-1):
    return jax.nn.softmax(x, axis=axis)

def _gelu(x):
    return jax.nn.gelu(x, approximate=True)

def _silu(x):
    return jax.nn.silu(x)

def _sigmoid(x):
    return jax.nn.sigmoid(x)

def _layernorm(x, axis=-1, eps=1e-05):
    m = jnp.mean(x, axis=axis, keepdims=True)
    v = jnp.var(x, axis=axis, keepdims=True)
    return (x - m) / jnp.sqrt(v + eps)

def _scatter_add(tgt, idx, src, axis=0):
    return tgt.at[idx].add(src)

def _segment_sum(src, seg, n):
    return jax.ops.segment_sum(src, seg, n)
kernel_name = 'mk_adaln_d1_jaxref_r8_1d4467'

def setup_inputs(seed: int=0):
    np.random.seed(seed)
    _w = jnp.asarray

    def _L0_attn_setup():
        import jax, jax.numpy as jnp
        import numpy as np
        NUM_HEADS = 16
        key = jax.random.key(seed)
        ks = jax.random.split(key, 9)
        B, S, D, H = (4, 256, 128, 128)
        s = 0.02
        return {'x': jax.random.normal(ks[0], (B, S, D), jnp.float32), 'Wq': jax.random.normal(ks[1], (D, H), jnp.float32) * s, 'bq': jax.random.normal(ks[2], (H,), jnp.float32) * s, 'Wk': jax.random.normal(ks[3], (D, H), jnp.float32) * s, 'bk': jax.random.normal(ks[4], (H,), jnp.float32) * s, 'Wv': jax.random.normal(ks[5], (D, H), jnp.float32) * s, 'bv': jax.random.normal(ks[6], (H,), jnp.float32) * s, 'Wmix': jax.random.normal(ks[7], (H, H), jnp.float32) * s, 'bmix': jax.random.normal(ks[8], (H,), jnp.float32) * s}
    _L0_attn_in = _L0_attn_setup()

    def _L0_ffn_setup():
        import jax, jax.numpy as jnp
        import numpy as np
        B, S, D = (8, 64, 128)
        H = 16
        DFF = 512
        E = 4
        K = 2
        EPS = 1e-05

        def _layernorm(x, w, b):
            m = x.mean(-1, keepdims=True)
            v = ((x - m) ** 2).mean(-1, keepdims=True)
            return (x - m) / jnp.sqrt(v + EPS) * w + b

        def _encoder_layer(x, iw, ib, ow, ob, l1w, l1b, l2w, l2b, n1w, n1b, n2w, n2b):
            b, s, d = x.shape
            hd = d // H
            qkv = x @ iw.T + ib
            q, k, v = jnp.split(qkv, 3, axis=-1)
            rs = lambda t: t.reshape(b, s, H, hd).transpose(0, 2, 1, 3)
            q, k, v = (rs(q), rs(k), rs(v))
            scale = jnp.asarray(hd, x.dtype) ** 0.5
            scores = jnp.einsum('bhqd,bhkd->bhqk', q, k) / scale
            attn = jax.nn.softmax(scores, axis=-1)
            o = jnp.einsum('bhqk,bhkd->bhqd', attn, v).transpose(0, 2, 1, 3).reshape(b, s, d)
            o = o @ ow.T + ob
            x = _layernorm(x + o, n1w, n1b)
            ff = jax.nn.relu(x @ l1w.T + l1b) @ l2w.T + l2b
            return _layernorm(x + ff, n2w, n2b)
        key = jax.random.key(seed)
        ks = jax.random.split(key, 12)
        g = lambda k, shape: jax.random.normal(k, shape, dtype=jnp.float32) * 0.02
        return {'x': jax.random.normal(ks[0], (B, S, D), dtype=jnp.float32), 'in_proj_w': g(ks[1], (E, 3 * D, D)), 'in_proj_b': g(ks[2], (E, 3 * D)), 'out_proj_w': g(ks[3], (E, D, D)), 'out_proj_b': g(ks[4], (E, D)), 'ln1_w': jnp.ones((E, D), jnp.float32), 'ln1_b': jnp.zeros((E, D), jnp.float32), 'lin1_w': g(ks[5], (E, DFF, D)), 'lin1_b': g(ks[6], (E, DFF)), 'lin2_w': g(ks[7], (E, D, DFF)), 'lin2_b': g(ks[8], (E, D)), 'ln2_w': jnp.ones((E, D), jnp.float32), 'ln2_b': jnp.zeros((E, D), jnp.float32), 'gate_w': g(ks[9], (E, D)), 'gate_b': g(ks[10], (E,))}
    _L0_ffn_in = _L0_ffn_setup()
    _L0_c = _w((lambda *s: np.random.randn(*s).astype(np.float32) * 0.05)(4, 128))
    _L0_wmod = _w((lambda *s: np.random.randn(*s).astype(np.float32) * 0.05)(128, 6 * 128) * 128 ** (-0.5))
    _d = {'L0_attn_x': _L0_attn_in['x'], 'L0_attn_Wq': _L0_attn_in['Wq'], 'L0_attn_bq': _L0_attn_in['bq'], 'L0_attn_Wk': _L0_attn_in['Wk'], 'L0_attn_bk': _L0_attn_in['bk'], 'L0_attn_Wv': _L0_attn_in['Wv'], 'L0_attn_bv': _L0_attn_in['bv'], 'L0_attn_Wmix': _L0_attn_in['Wmix'], 'L0_attn_bmix': _L0_attn_in['bmix'], 'L0_ffn_in_proj_w': _L0_ffn_in['in_proj_w'], 'L0_ffn_in_proj_b': _L0_ffn_in['in_proj_b'], 'L0_ffn_out_proj_w': _L0_ffn_in['out_proj_w'], 'L0_ffn_out_proj_b': _L0_ffn_in['out_proj_b'], 'L0_ffn_ln1_w': _L0_ffn_in['ln1_w'], 'L0_ffn_ln1_b': _L0_ffn_in['ln1_b'], 'L0_ffn_lin1_w': _L0_ffn_in['lin1_w'], 'L0_ffn_lin1_b': _L0_ffn_in['lin1_b'], 'L0_ffn_lin2_w': _L0_ffn_in['lin2_w'], 'L0_ffn_lin2_b': _L0_ffn_in['lin2_b'], 'L0_ffn_ln2_w': _L0_ffn_in['ln2_w'], 'L0_ffn_ln2_b': _L0_ffn_in['ln2_b'], 'L0_ffn_gate_w': _L0_ffn_in['gate_w'], 'L0_ffn_gate_b': _L0_ffn_in['gate_b'], 'L0_c': _L0_c, 'L0_wmod': _L0_wmod}
    _x0 = _d['L0_attn_x']
    _d['L0_attn_x'] = jax.random.normal(jax.random.fold_in(jax.random.key(seed), 1), (4, 512, 128), dtype=_x0.dtype)
    del _x0
    return _d

def reference(L0_attn_x, L0_attn_Wq, L0_attn_bq, L0_attn_Wk, L0_attn_bk, L0_attn_Wv, L0_attn_bv, L0_attn_Wmix, L0_attn_bmix, L0_ffn_in_proj_w, L0_ffn_in_proj_b, L0_ffn_out_proj_w, L0_ffn_out_proj_b, L0_ffn_ln1_w, L0_ffn_ln1_b, L0_ffn_lin1_w, L0_ffn_lin1_b, L0_ffn_lin2_w, L0_ffn_lin2_b, L0_ffn_ln2_w, L0_ffn_ln2_b, L0_ffn_gate_w, L0_ffn_gate_b, L0_c, L0_wmod):

    def _L0_attn_ref(x, Wq, bq, Wk, bk, Wv, bv, Wmix, bmix):
        import jax, jax.numpy as jnp
        import numpy as np
        NUM_HEADS = 16
        B, S, _ = x.shape
        nh = NUM_HEADS
        hd = Wq.shape[1] // nh
        scale = hd ** 0.5

        def heads(W, b):
            return (x @ W + b).reshape(B, S, nh, hd).transpose(0, 2, 1, 3)
        q, k, v = (heads(Wq, bq), heads(Wk, bk), heads(Wv, bv))
        scores = jnp.einsum('bhqd,bhkd->bhqk', q, k) / scale
        causal = jnp.tril(jnp.ones((S, S), bool))
        scores = jnp.where(causal, scores, -jnp.inf)
        probs = jax.nn.softmax(scores, axis=-1)
        att = jnp.einsum('bhqk,bhkd->bhqd', probs, v)
        att = att.transpose(0, 2, 1, 3).reshape(B, S, nh * hd)
        return att @ Wmix + bmix

    def _L0_ffn_ref(x, in_proj_w, in_proj_b, out_proj_w, out_proj_b, ln1_w, ln1_b, lin1_w, lin1_b, lin2_w, lin2_b, ln2_w, ln2_b, gate_w, gate_b):
        import jax, jax.numpy as jnp
        import numpy as np
        B, S, D = (8, 64, 128)
        H = 16
        DFF = 512
        E = 4
        K = 2
        EPS = 1e-05

        def _layernorm(x, w, b):
            m = x.mean(-1, keepdims=True)
            v = ((x - m) ** 2).mean(-1, keepdims=True)
            return (x - m) / jnp.sqrt(v + EPS) * w + b

        def _encoder_layer(x, iw, ib, ow, ob, l1w, l1b, l2w, l2b, n1w, n1b, n2w, n2b):
            b, s, d = x.shape
            hd = d // H
            qkv = x @ iw.T + ib
            q, k, v = jnp.split(qkv, 3, axis=-1)
            rs = lambda t: t.reshape(b, s, H, hd).transpose(0, 2, 1, 3)
            q, k, v = (rs(q), rs(k), rs(v))
            scale = jnp.asarray(hd, x.dtype) ** 0.5
            scores = jnp.einsum('bhqd,bhkd->bhqk', q, k) / scale
            attn = jax.nn.softmax(scores, axis=-1)
            o = jnp.einsum('bhqk,bhkd->bhqd', attn, v).transpose(0, 2, 1, 3).reshape(b, s, d)
            o = o @ ow.T + ob
            x = _layernorm(x + o, n1w, n1b)
            ff = jax.nn.relu(x @ l1w.T + l1b) @ l2w.T + l2b
            return _layernorm(x + ff, n2w, n2b)
        gate_logits = x.mean(axis=1) @ gate_w.T + gate_b
        _, top_idx = jax.lax.top_k(gate_logits, K)
        gate_weights = jax.nn.softmax(gate_logits, axis=-1)
        mask = jnp.zeros_like(gate_weights).at[jnp.arange(x.shape[0])[:, None], top_idx].set(1.0)
        expert_outs = jax.vmap(_encoder_layer, in_axes=(None, 0, 0, 0, 0, 0, 0, 0, 0, 0, 0, 0, 0))(x, in_proj_w, in_proj_b, out_proj_w, out_proj_b, lin1_w, lin1_b, lin2_w, lin2_b, ln1_w, ln1_b, ln2_w, ln2_b)
        return jnp.einsum('be,ebsd->bsd', gate_weights * mask, expert_outs)
    x = L0_attn_x
    mod = (_silu(L0_c) @ L0_wmod).reshape(L0_c.shape[0], 6, 1, -1)
    sa, ca, ga, sb, cb, gb = (mod[:, 0], mod[:, 1], mod[:, 2], mod[:, 3], mod[:, 4], mod[:, 5])
    ga = (2 * (ga >= 0) - 1) * jnp.maximum(jnp.abs(ga), 0.25)
    gb = (2 * (gb >= 0) - 1) * jnp.maximum(jnp.abs(gb), 0.25)
    h = _layernorm(x, axis=-1) * (1 + ca) + sa
    x = x + ga * _L0_attn_ref(h, L0_attn_Wq, L0_attn_bq, L0_attn_Wk, L0_attn_bk, L0_attn_Wv, L0_attn_bv, L0_attn_Wmix, L0_attn_bmix)
    h = _layernorm(x, axis=-1) * (1 + cb) + sb
    x = x + gb * _L0_ffn_ref(h, L0_ffn_in_proj_w, L0_ffn_in_proj_b, L0_ffn_out_proj_w, L0_ffn_out_proj_b, L0_ffn_ln1_w, L0_ffn_ln1_b, L0_ffn_lin1_w, L0_ffn_lin1_b, L0_ffn_lin2_w, L0_ffn_lin2_b, L0_ffn_ln2_w, L0_ffn_ln2_b, L0_ffn_gate_w, L0_ffn_gate_b)
    return x

_drawn_inputs = setup_inputs


def setup_inputs(seed=0):
    import zlib

    import numpy as np

    out = dict(_drawn_inputs(seed))
    spreads = {'L0_ffn_ln1_w': (1.0, 0.6),
     'L0_ffn_ln1_b': (0.0, 0.8),
     'L0_ffn_ln2_w': (1.0, 0.6),
     'L0_ffn_ln2_b': (0.0, 0.8)}
    factors = {'L0_attn_Wq': 8.0,
     'L0_attn_bq': 8.0,
     'L0_attn_Wk': 8.0,
     'L0_attn_bk': 200.0,
     'L0_attn_Wv': 8.0,
     'L0_attn_bv': 8.0,
     'L0_attn_Wmix': 8.0,
     'L0_attn_bmix': 8.0,
     'L0_ffn_in_proj_w': 8.0,
     'L0_ffn_in_proj_b': 22.884,
     'L0_ffn_out_proj_w': 8.0,
     'L0_ffn_out_proj_b': 60.701,
     'L0_ffn_lin1_w': 8.0,
     'L0_ffn_lin1_b': 64.0,
     'L0_ffn_lin2_w': 8.0,
     'L0_ffn_lin2_b': 200.0}
    for name, (base, spread) in spreads.items():
        noise = np.random.default_rng([zlib.crc32(name.encode()), seed]).standard_normal(out[name].shape)
        drawn = base * np.exp(spread * noise) if base else spread * noise
        out[name] = jnp.asarray(drawn.astype(out[name].dtype))
    for name, factor in factors.items():
        out[name] = (out[name] * factor).astype(out[name].dtype)
    return out
```

```python
from contextlib import ExitStack

import concourse.bass as bass
from concourse import mybir

F32 = mybir.dt.float32
BF16 = mybir.dt.bfloat16
I32 = mybir.dt.int32
ALU = mybir.AluOpType
ACT = mybir.ActivationFunctionType
AX = mybir.AxisListType

P = 128
NB, S, D = 4, 512, 128
HD = 8
T = S // P
NE, TOPK, FF = 4, 2, 512
FC = FF // P
NQ = 4
NJ = 4
PARTS = 3
KROWS = PARTS * PARTS * HD
KALL = KROWS + PARTS
VW = 16
TICKS = NQ * T
PBUF = 4
EPS = 1e-5
SCALE = HD ** -0.5
MASKED = -1e30
NA = NB
NU = NA + NB * TOPK
W_IN, W_POST = 3 * D + 2, D + FF + FC * D + FC
DMA = 16


def kind(u):
    return "A" if u < NA else "B"


ATTN_ITEMS = [(0, 0, "off1"), (0, 0, "stk3"), (1, 0, "vp3"), (4, 0, "off2"), (8, 0, "off3")]
PREP_ITEMS = {
    "A": [(0, 0, "loadA"), (0, 1, "ln1a"), (1, 0, "ln1b"), (1, 1, "hT"), (2, 1, "q"), (3, 1, "k"),
          (4, 1, "v"), (4, 1, "scr")],
    "B": [(0, 0, "loadB"), (1, 1, "q"), (2, 1, "k"), (3, 1, "v"), (3, 1, "scr")],
    "all": [(5, 0, "stk0"), (5, 1, "vp0"), (8, 0, "stk1"), (9, 0, "vp1"), (12, 0, "stk2"), (12, 0, "off0"),
            (13, 0, "vp2")],
}
POST_ITEMS = {
    "A": [(0, 0, "loadPA"), (1, 0, "O0"), (2, 0, "O1"), (3, 0, "aT"), (4, 1, "opA"), (5, 0, "ln2"),
          (6, 0, "h2T"), (6, 1, "gsum"), (7, 0, "gate")],
    "B": [(0, 0, "loadPB"), (1, 0, "O0"), (2, 0, "O1"), (3, 0, "aT"), (4, 1, "opB"), (5, 0, "ln3"),
          (6, 0, "x1T"), (7, 0, "ff0"), (8, 1, "ff1"), (9, 1, "ff2"), (10, 1, "ff3"), (11, 1, "out"),
          (12, 1, "ln4")],
}
MISC = ("off0", "off1", "off2", "off3", "hT", "q", "k", "v", "O0", "O1", "aT", "opA", "opB", "h2T",
        "gate", "x1T", "ff0", "ff1", "ff2", "ff3", "out")


class Body:

    def __init__(self, first, count, misc_base):
        self.first, self.count, self.misc_base = first, count, misc_base
        u = first
        self.steps = kind(u) if 0 <= u < NU else None
        self.prep = kind(u + 1) if u + 1 < NU else None
        self.post = kind(u - 1) if 0 <= u - 1 < NU else None
        items = []
        if self.prep:
            items += PREP_ITEMS[self.prep] + PREP_ITEMS["all"]
        if self.steps:
            items += ATTN_ITEMS
        if self.post:
            items += POST_ITEMS[self.post]
        self.items = sorted(items, key=lambda i: (i[0], i[1]))
        self.misc = [n for _, _, n in self.items if n in MISC]

    def at(self, u):
        self.u = u
        self.misc_now = self.misc_base + (u - self.first) * len(self.misc)
        return self

    def misc_use(self, name):
        return self.misc_now + self.misc.index(name)


def bodies():
    out, base = [], 0
    for first, count in ((-1, 1), (0, 1), (1, 2), (3, 1), (4, 1), (5, NU - 6), (NU - 1, 1), (NU, 1)):
        out.append(Body(first, count, base))
        base += count * len(out[-1].misc)
    return out


def walk(eng, half_step, item, pv_step):
    def emit(b):
        for tick in range(TICKS):
            for half in range(2):
                half_step(b, tick, half)
                for t, h, name in b.items:
                    if (t, h) == (tick, half):
                        item(b, name)
            pv_step(b, tick)

    for b in bodies():
        if b.count == 1:
            emit(b.at(b.first))
        else:
            with eng.Fori(b.first, b.first + b.count) as u:
                emit(b.at(u))


def adaln_kernel(nc, x, w_attn, cols_attn, rows_attn, w_exp, rows_exp, gate_wT, gate_b, cT, wmod, out):
    ctx = ExitStack()
    with ctx:
        def sb(name, shape, dt=F32):
            return ctx.enter_context(nc.sbuf_tensor(name, shape, dt))

        def pb(name, shape, dt=F32):
            return ctx.enter_context(nc.psum_tensor(name, shape, dt))

        def sem(name):
            return ctx.enter_context(nc.semaphore(name))

        kstk = sb("kstk", [P, NQ * NJ, S], BF16)
        qstk = sb("qstk", [P, NQ * NJ, S], BF16)
        probs = sb("probs", [P, PBUF, NJ, S])
        vpad = sb("vpad", [P, T, NQ, NJ, 2 * VW])
        v_sb = sb("v_sb", [P, T, D])
        att_u = sb("att_u", [P, 2, S])
        h_sb = sb("h_sb", [P, T, D])
        h_T = sb("h_T", [P, S])
        q_f = sb("q_f", [P, S])
        k_f = sb("k_f", [P, S])
        q_r = sb("q_r", [P, S])
        k_r = sb("k_r", [P, S])
        q_parts = sb("q_parts", [P, PARTS, S], BF16)
        k_parts = sb("k_parts", [P, PARTS, S], BF16)
        row_max = sb("row_max", [P, 2, T, NJ])
        max_r = sb("max_r", [P, 2, T, NJ])
        max_parts = sb("max_parts", [P, 2, T, PARTS, NJ], BF16)
        off_rows = sb("off_rows", [PARTS * NJ, 2, S], BF16)
        w_a = sb("w_a", [P, 4 * D])
        cols_a = sb("cols_a", [P, 2])
        rows_a = sb("rows_a", [P, 2, D])
        w_in = sb("w_in", [P, W_IN])
        bv_in = sb("bv_in", [P, D])
        w_post = sb("w_post", [P, W_POST])
        rows_post = sb("rows_post", [P, 6, D])
        x_in = sb("x_in", [P, T, D])
        mod_in = sb("mod_in", [P, 2, D])
        mod_c = sb("mod_c", [P, D])
        x_post = sb("x_post", [P, T, D])
        mod_post = sb("mod_post", [P, 3, D])
        mod_p1 = sb("mod_p1", [P, D])
        gb_post = sb("gb_post", [P, D])
        h2_post = sb("h2_post", [P, T, D])
        recip = sb("recip", [P, 2, 2 * NQ * NJ])
        attn = sb("attn", [P, T, D])
        attn_T = sb("attn_T", [P, S])
        t1 = sb("t1", [P, T, D])
        t2 = sb("t2", [P, T, D])
        x2 = sb("x2", [P, T, D])
        h2 = sb("h2", [P, T, D])
        h2_T = sb("h2_T", [P, S])
        x1 = sb("x1", [P, T, D])
        x1_T = sb("x1_T", [P, S])
        hid = sb("hid", [P, FC, S])
        y = sb("y", [P, T, D])
        acc = sb("acc", [P, T, D])
        stats = sb("stats", [P, 4, T, 6])
        mv = sb("mv", [P, 4, T, 2])
        var_e = sb("var_e", [P, 4, T])
        rstd0 = sb("rstd0", [P, 4, T])
        newton = sb("newton", [P, 4, 2, T])
        minus_half = sb("minus_half", [P, T])
        rstd = sb("rstd", [P, 4, T])
        h_sum = sb("h_sum", [P, 1])
        h_sum_b = sb("h_sum_b", [P, P])
        gw = sb("gw", [P, NE])
        gb_b = sb("gb_b", [P, NE])
        before = sb("before", [P, NE, NE])
        e_no = sb("e_no", [P, NE])
        lg = sb("lg", [P, NE])
        lmax = sb("lmax", [P, 1])
        lsh = sb("lsh", [P, NE])
        lexp = sb("lexp", [P, NE])
        lsum = sb("lsum", [P, 1])
        lrec = sb("lrec", [P, 1])
        gt = sb("gt", [P, NE, NE])
        eq = sb("eq", [P, NE, NE])
        rank = sb("rank", [P, NE])
        pick = sb("pick", [P, TOPK, NE])
        pick_w = sb("pick_w", [P, TOPK, NE])
        pick_n = sb("pick_n", [P, TOPK, NE])
        nsel_f = sb("nsel_f", [P, TOPK])
        wsel = sb("wsel", [P, NB * TOPK])
        nsel = sb("nsel", [P, NB * TOPK], I32)
        gate_q = sb("gate_q", [P, 1])
        c_T = sb("c_T", [P, NB])
        c_e = sb("c_e", [P, NB])
        c_s = sb("c_s", [P, NB])
        w_mod = sb("w_mod", [P, 6 * D])
        mod4 = sb("mod4", [NB, 6, D])
        mod_a = sb("mod_a", [NB, 2, D])
        mod_s = sb("mod_s", [NB, 2, D])
        zeros = sb("zeros", [P, P])
        id_f = sb("id_f", [P, P])
        id_b = sb("id_b", [P, P], BF16)
        mask_q = sb("mask_q", [P, P], BF16)
        mask_k = sb("mask_k", [P, P], BF16)
        neg = sb("neg", [P, P], BF16)

        st_ps = pb("st_ps", [P, 4, S])
        s_ps = pb("s_ps", [P, 2, S])
        pv_ps = pb("pv_ps", [P, S])
        misc = pb("misc", [P, S])
        misc_b = misc[:, :].bitcast(BF16)
        misc_t = misc[:, :].rearrange("p (t d) -> p t d", t=T)

        stk_shape = [NQ * NJ, PARTS, PARTS, HD, S]
        q_dram = nc.dram_tensor("q_scratch", stk_shape, BF16).ap()
        k_dram = nc.dram_tensor("k_scratch", stk_shape, BF16).ap()
        mod_dram = nc.dram_tensor("mod_scratch", [NB, 6 * D], F32).ap()
        h2_dram = nc.dram_tensor("h2_scratch", [NB, S, D], F32).ap()
        h2T_dram = nc.dram_tensor("h2T_scratch", [NB, P, S], F32).ap()

        def tokens(a):
            return a.rearrange("(t p) d -> p t d", p=P)

        q_rows = q_dram.rearrange("(gp j sub) a i d n -> gp sub (a i d) j n", gp=2, j=NJ)
        k_rows = k_dram.rearrange("(gp j sub) a i d n -> gp sub (a i d) j n", gp=2, j=NJ)

        consts_in = sem("consts_in")
        cmod_in = sem("cmod_in")
        consts_made = sem("consts_made")
        ones_made = sem("ones_made")
        setup_chain = sem("setup_chain")
        setup_pool = sem("setup_pool")
        silu_exp = sem("silu_exp")
        silu_made = sem("silu_made")
        mod_mm = sem("mod_mm")
        mod_made = sem("mod_made")
        mod_out = sem("mod_out")
        st_full = sem("st_full")
        exp_done = sem("exp_done")
        s_full = sem("s_full")
        max_done = sem("max_done")
        parts_ready = sem("parts_ready")
        parts_chain = sem("parts_chain")
        off_in = [sem(f"off{g}_in") for g in range(NQ)]
        pv_done = sem("pv_done")
        ev_done = sem("ev_done")
        misc_full = sem("misc_full")
        misc_free = sem("misc_free")
        ln1_chain = sem("ln1_chain")
        ln2_chain = sem("ln2_chain")
        ln3_chain = sem("ln3_chain")
        ln4_chain = sem("ln4_chain")
        var_ready = [sem(f"var{i}_ready") for i in range(4)]
        pow_ready = [sem(f"pow{i}_ready") for i in range(4)]
        h_ready = sem("h_ready")
        q_chain = sem("q_chain")
        k_chain = sem("k_chain")
        q_split = sem("q_split")
        k_split = sem("k_split")
        scr_out = sem("scr_out")
        stk_in = [sem(f"stk{g}_in") for g in range(NQ)]
        vpad_ready = sem("vpad_ready")
        pa_in = sem("pa_in")
        pb_in = sem("pb_in")
        qa_in = sem("qa_in")
        qb_in = sem("qb_in")
        rec_done = sem("rec_done")
        x2_ready = sem("x2_ready")
        h2_ready = sem("h2_ready")
        hsum_ready = sem("hsum_ready")
        gate_chain = sem("gate_chain")
        lsh_ready = sem("lsh_ready")
        lexp_ready = sem("lexp_ready")
        sel_ready = sem("sel_ready")
        a_out = sem("a_out")
        x1_ready = sem("x1_ready")
        acc_ready = sem("acc_ready")
        b_out = sem("b_out")

        LOADS = {"pa": 2, "pb": 3, "qa": 2, "qb": 5, "a_out": 3, "const": 5, "scr": 2 * PARTS * PARTS}

        block = ctx.enter_context(nc.Block())

        def wait(eng, s, value, bare=False):
            if isinstance(value, int):
                if value > 0:
                    eng.wait_ge(s, value)
                return
            if bare or eng.engine == nc.sync.engine:
                value = eng.to_reg(value)
                true_since_setup, n = {nc.sync.engine: (mod_out, DMA), nc.gpsimd.engine: (consts_made, 1),
                                       nc.vector.engine: (ones_made, 1)}[eng.engine]
                eng.wait_ge(true_since_setup, n)
            eng.wait_ge(s, value)

        class Chain:

            def __init__(self, eng, s, per, unit):
                self.eng, self.s, self.per, self.base, self.n = eng, s, per, unit * per, 0

            def link(self, ins, bare_next=False):
                self.n += 1
                ins.then_inc(self.s, 1)
                wait(self.eng, self.s, self.base + self.n, bare_next)

            def end(self):
                assert self.n == self.per, (self.n, self.per)

        @block.sync
        def _(sp):
            sp.dma_start(c_T[:, :], cT).then_inc(cmod_in, DMA)
            sp.dma_start(w_mod[:, :], wmod).then_inc(cmod_in, DMA)
            sp.dma_start(w_a[:, :], w_attn).then_inc(consts_in, DMA)
            sp.dma_start(cols_a[:, :], cols_attn).then_inc(consts_in, DMA)
            sp.dma_start(rows_a[:, :, :], rows_attn.partition_broadcast(P)).then_inc(consts_in, DMA)
            sp.dma_start(gw[:, :], gate_wT).then_inc(consts_in, DMA)
            sp.dma_start(gb_b[:, :], gate_b.partition_broadcast(P)).then_inc(consts_in, DMA)
            sp.wait_ge(mod_made, 1)
            sp.dma_start(mod_dram, mod4[:, :, :].rearrange("b m d -> b (m d)")).then_inc(mod_out, DMA)
            sp.wait_ge(mod_out, DMA)

            def half_step(b, tick, half):
                pass

            def pv_step(b, tick):
                pass

            def load_stack(v, g):
                wait(sp, st_full, (v - 1) * 2 * TICKS + 2 * T * (g + 1))
                wait(sp, s_full, (v - 1) * NJ * TICKS + NJ * T * (g + 1))
                for dst, src in ((qstk, q_rows), (kstk, k_rows)):
                    sp.dma_start(dst[0:KROWS, NJ * g:NJ * g + NJ, :], src[g // 2, g % 2]).then_inc(stk_in[g], DMA)

            def load_off(b, v, g, name):
                wait(sp, misc_free, b.misc_use(name) + 1)
                sp.dma_start(qstk[KROWS:KALL, NJ * g:NJ * g + NJ, :], off_rows[:, g % 2, :]).then_inc(off_in[g], DMA)

            def item(b, name):
                u = b.u
                if name == "stk3":
                    load_stack(u, 3)
                elif name in ("stk0", "stk1", "stk2"):
                    load_stack(u + 1, int(name[3]))
                elif name == "off0":
                    load_off(b, u + 1, 0, name)
                elif name in ("off1", "off2", "off3"):
                    load_off(b, u, int(name[3]), name)
                elif name == "loadA":
                    v = u + 1
                    wait(sp, h_ready, v)
                    sp.dma_start(x_in[:, :, :], tokens(x[v])).then_inc(pa_in, DMA)
                    sp.dma_start(mod_in[:, :, :].rearrange("p m d -> p (m d)"),
                                 mod_dram[v, 0:2 * D].partition_broadcast(P)).then_inc(pa_in, DMA)
                elif name == "loadB":
                    w = u + 1 - NA
                    wait(sp, sel_ready, w // TOPK + 1)
                    wait(sp, a_out, (w // TOPK + 1) * LOADS["a_out"] * DMA)
                    e = sp.value_load(nsel[0:1, bass.ds(w, 1)], min_val=0, max_val=NE - 1)
                    wait(sp, vpad_ready, (w + NA) * NQ - 1)
                    sp.dma_start(h_T[:, :], h2T_dram[w // TOPK]).then_inc(pb_in, DMA)
                    sp.dma_start(w_in[:, :], w_exp[e, :, 0:W_IN]).then_inc(pb_in, DMA)
                    sp.dma_start(bv_in[:, :], rows_exp[e, 0:D].partition_broadcast(P)).then_inc(pb_in, DMA)
                elif name == "scr":
                    v = u + 1
                    for g in range(NQ):
                        wait(sp, stk_in[g], v * 2 * DMA)
                    wait(sp, q_split, v + 1)
                    for i in range(PARTS):
                        for a in range(PARTS):
                            sp.dma_start(q_dram[:, a, i], q_parts[:, i, :]).then_inc(scr_out, DMA)
                    wait(sp, k_split, v + 1)
                    for a in range(PARTS):
                        for i in range(PARTS):
                            sp.dma_start(k_dram[:, a, i], k_parts[:, a, :]).then_inc(scr_out, DMA)
                    wait(sp, scr_out, (v + 1) * LOADS["scr"] * DMA)
                elif name == "loadPA":
                    v = u - 1
                    wait(sp, sel_ready, v)
                    sp.dma_start(x_post[:, :, :], tokens(x[v])).then_inc(qa_in, DMA)
                    sp.dma_start(mod_post[:, :, :].rearrange("p m d -> p (m d)"),
                                 mod_dram[v, 2 * D:5 * D].partition_broadcast(P)).then_inc(qa_in, DMA)
                elif name == "loadPB":
                    w = u - 1 - NA
                    wait(sp, a_out, NA * LOADS["a_out"] * DMA) if isinstance(w, int) and w == 0 else wait(sp, b_out, w * DMA)
                    e = sp.value_load(nsel[0:1, bass.ds(w, 1)], min_val=0, max_val=NE - 1)
                    sp.dma_start(w_post[:, :], w_exp[e, :, W_IN:W_IN + W_POST]).then_inc(qb_in, DMA)
                    sp.dma_start(rows_post[:, :, :].rearrange("p m d -> p (m d)"),
                                 rows_exp[e, D:7 * D].partition_broadcast(P)).then_inc(qb_in, DMA)
                    sp.dma_start(gb_post[:, :], mod_dram[w // TOPK, 5 * D:6 * D].partition_broadcast(P)).then_inc(qb_in, DMA)
                    sp.dma_start(h2_post[:, :, :], tokens(h2_dram[w // TOPK])).then_inc(qb_in, DMA)
                    sp.dma_start(x_post[:, :, :], tokens(out[w // TOPK])).then_inc(qb_in, DMA)
                elif name == "h2T":
                    v = u - 1
                    wait(sp, h2_ready, v + 1)
                    sp.dma_start(tokens(out[v]), x2[:, :, :]).then_inc(a_out, DMA)
                    sp.dma_start(tokens(h2_dram[v]), h2[:, :, :]).then_inc(a_out, DMA)
                    wait(sp, misc_free, b.misc_use(name) + 1)
                    sp.dma_start(h2T_dram[v], h2_T[:, :]).then_inc(a_out, DMA)
                elif name == "ln4":
                    w = u - 1 - NA
                    wait(sp, acc_ready, w + 1)
                    sp.dma_start(tokens(out[w // TOPK]), acc[:, :, :]).then_inc(b_out, DMA)

            walk(sp, half_step, item, pv_step)
            sp.wait_ge(b_out, NB * TOPK * DMA)

        @block.gpsimd
        def _(pool):
            chain = Chain(pool, setup_pool, 7, 0)
            chain.link(nc.gpsimd.memset(id_f[:, :], 0.0))
            chain.link(nc.gpsimd.memset(zeros[:, :], 0.0))
            chain.link(nc.gpsimd.affine_select(out=id_f[:, :], in_=id_f[:, :], compare_op=ALU.not_equal, fill=1.0,
                                               base=0, pattern=[[-1, P]], channel_multiplier=1))
            chain.link(nc.gpsimd.tensor_copy(id_b[:, :], id_f[:, :]))
            chain.link(nc.gpsimd.affine_select(out=neg[:, :], in_=zeros[:, :], compare_op=ALU.is_ge, fill=MASKED,
                                               base=0, pattern=[[-1, P]], channel_multiplier=1))
            chain.link(nc.gpsimd.tensor_copy(mask_q[:, :], neg[:, :]))
            chain.link(nc.gpsimd.affine_select(out=mask_k[:, :], in_=zeros[:, :], compare_op=ALU.is_ge, fill=MASKED,
                                               base=0, pattern=[[1, P]], channel_multiplier=-1))
            chain.end()
            nc.gpsimd.memset(minus_half[:, :], -0.5).then_inc(consts_made, 1)
            pool.wait_ge(consts_made, 1)

            def half_step(b, tick, half):
                pass

            def pv_step(b, tick):
                pass

            def power(i, unit):
                pool.wait_ge(var_ready[i], unit + 1)
                nc.gpsimd.tensor_tensor(rstd0[:, i, :], var_e[:, i, :], minus_half[:, :], ALU.pow)\
                  .then_inc(pow_ready[i], 1)

            def place_v(v, g):
                gp, sub = g // 2, g % 2
                wait(pool, pv_done, (v - 1) * TICKS + T * (g + 1), bare=True)
                nc.gpsimd.tensor_copy(
                    vpad[:, :, g, :, sub * VW:sub * VW + HD],
                    v_sb[:, :, :].rearrange("p k (gp j sub d) -> p k gp j sub d", gp=2, j=NJ, sub=2)[:, :, gp, :, sub, :],
                ).then_inc(vpad_ready, 1)

            def item(b, name):
                u = b.u
                if name == "ln1a":
                    power(0, u + 1)
                elif name == "opA":
                    power(1, u - 1)
                elif name == "opB":
                    power(2, u - 1 - NA)
                elif name == "out":
                    power(3, u - 1 - NA)
                elif name == "k":
                    v = u + 1
                    wait(pool, misc_free, b.misc_use("k") + 1, bare=True)
                    wait(pool, scr_out, v * LOADS["scr"] * DMA, bare=True)
                    chain = Chain(pool, k_chain, 3, v)
                    chain.link(nc.gpsimd.tensor_copy(k_parts[:, 0, :], k_f[:, :]))
                    chain.link(nc.gpsimd.tensor_tensor(k_r[:, :], k_f[:, :], k_parts[:, 0, :], ALU.subtract), bare_next=True)
                    chain.link(nc.gpsimd.tensor_copy(k_parts[:, 1, :], k_r[:, :]))
                    chain.end()
                    nc.gpsimd.tensor_tensor(k_parts[:, 2, :], k_r[:, :], k_parts[:, 1, :], ALU.subtract)\
                      .then_inc(k_split, 1)
                elif name == "vp3":
                    place_v(u, 3)
                elif name in ("vp0", "vp1", "vp2"):
                    if name == "vp0":
                        wait(pool, misc_free, b.misc_use("v") + 1, bare=True)
                        wait(pool, ones_made, 1)
                    place_v(u + 1, int(name[2]))

            walk(pool, half_step, item, pv_step)

        @block.scalar
        def _(act):
            act.wait_ge(cmod_in, 2 * DMA)
            nc.scalar.activation(c_e[:, :], c_T[:, :], ACT.Exp, scale=-1.0).then_inc(silu_exp, 1)

            def half_step(b, tick, half):
                if not b.steps:
                    return
                n = b.u * 2 * TICKS + 2 * tick + half
                key = tick % T
                lo = key * P if b.steps == "A" else 0
                act.wait_ge(st_full, n + 1)
                wait(act, pv_done, b.u * TICKS + tick - (PBUF - 1))
                nc.scalar.activation(probs[:, tick % PBUF, 2 * half:2 * half + 2, lo:S],
                                     st_ps[:, 2 * half:2 * half + 2, lo:S], ACT.Exp, scale=SCALE)\
                  .then_inc(exp_done, 1)

            def pv_step(b, tick):
                gp = {8: 0, 0: 1}.get(tick)
                if gp is None or (gp == 0 and not b.steps) or (gp == 1 and not b.post):
                    return
                unit = b.u if gp == 0 else b.u - 1
                act.wait_ge(pv_done, unit * TICKS + 8 * (gp + 1))
                nc.scalar.activation(att_u[:, gp, :], pv_ps[:, :], ACT.Copy).then_inc(ev_done, 1)

            def copy_off(b, v, g, name):
                act.wait_ge(misc_full, b.misc_use(name) + 1)
                wait(act, off_in[(g - 2) % NQ], (v + (g >= 2)) * DMA)
                nc.scalar.activation(off_rows[:, g % 2, :], misc_b[0:PARTS * NJ, 0:S], ACT.Copy).then_inc(misc_free, 1)

            def item(b, name):
                u = b.u
                if name == "off0":
                    copy_off(b, u + 1, 0, name)
                elif name in ("off1", "off2", "off3"):
                    copy_off(b, u, int(name[3]), name)
                elif name == "hT":
                    act.wait_ge(misc_full, b.misc_use(name) + 1)
                    nc.scalar.activation(h_T[:, :], misc[:, :], ACT.Copy).then_inc(misc_free, 1)
                elif name in ("q", "k"):
                    act.wait_ge(misc_full, b.misc_use(name) + 1)
                    col = 0 if name == "q" else 1
                    bias = cols_a if b.prep == "A" else w_in[:, 3 * D:W_IN]
                    dst = q_f if name == "q" else k_f
                    nc.scalar.activation(dst[:, :], misc[:, :], ACT.Identity, bias=bias[:, col:col + 1]).then_inc(misc_free, 1)
                elif name == "aT":
                    act.wait_ge(misc_full, b.misc_use(name) + 1)
                    nc.scalar.activation(attn_T[:, :], misc[:, :], ACT.Copy).then_inc(misc_free, 1)
                elif name == "h2T":
                    v = u - 1
                    act.wait_ge(misc_full, b.misc_use(name) + 1)
                    wait(act, a_out, v * DMA * LOADS["a_out"])
                    nc.scalar.activation(h2_T[:, :], misc[:, :], ACT.Identity, accum_out=h_sum[:, :]).then_inc(misc_free, 1)
                elif name == "gate":
                    act.wait_ge(lsh_ready, u)
                    nc.scalar.activation(lexp[:, :], lsh[:, :], ACT.Exp).then_inc(lexp_ready, 1)
                elif name == "x1T":
                    act.wait_ge(misc_full, b.misc_use(name) + 1)
                    nc.scalar.activation(x1_T[:, :], misc[:, :], ACT.Copy).then_inc(misc_free, 1)
                elif name in ("ff0", "ff1", "ff2", "ff3"):
                    c = int(name[2])
                    act.wait_ge(misc_full, b.misc_use(name) + 1)
                    nc.scalar.activation(hid[:, c, :], misc[:, :], ACT.Relu, bias=w_post[:, W_POST - FC + c:W_POST - FC + c + 1]).then_inc(misc_free, 1)

            walk(act, half_step, item, pv_step)

        @block.tensor
        def _(pe):
            pe.wait_ge(silu_made, 1)
            for i in range(2):
                w = 3 * D
                nc.tensor.matmul(s_ps[0:NB, i, 0:w], c_s[:, :], w_mod[:, i * w:(i + 1) * w], start=True, stop=True)\
                  .then_inc(mod_mm, 1)
            pe.wait_ge(consts_made, 1)
            pe.wait_ge(ones_made, 1)
            pe.wait_ge(consts_in, LOADS["const"] * DMA)
            pe.wait_ge(mod_made, 1)

            def score_tile(b, tick, c):
                knd, v = (b.steps, b.u) if tick < 8 else (b.prep, b.u + 1)
                if not knd:
                    return
                g = 2 + tick // T if tick < 8 else (tick - 8) // T
                t = tick % T
                n = b.u * NJ * TICKS + NJ * 8 + NJ * tick + c
                if t == 0 and c == 0:
                    pe.wait_ge(stk_in[g], (v + 1) * 2 * DMA)
                wait(pe, max_done, n - 1)
                bank = s_ps[:, c % 2, :]
                h = NJ * g + c
                keys = (t + 1) * P if knd == "A" else S
                ins = nc.tensor.matmul(bank[:, 0:keys], qstk[0:KROWS, h, t * P:(t + 1) * P], kstk[0:KROWS, h, 0:keys],
                                       start=True, stop=(knd == "B"))
                if knd == "A":
                    ins = nc.tensor.matmul(bank[:, t * P:keys], id_b[:, :], mask_q[:, :], start=False, stop=True)
                ins.then_inc(s_full, 1)

            def half_step(b, tick, half):
                if b.steps:
                    n = b.u * 2 * TICKS + 2 * tick + half
                    g, key = tick // T, tick % T
                    if key == 0 and half == 0:
                        pe.wait_ge(off_in[g], (b.u + 1) * DMA)
                    wait(pe, exp_done, n - 1)
                    lo = key * P if b.steps == "A" else 0
                    for j in (2 * half, 2 * half + 1):
                        h = NJ * g + j
                        ins = nc.tensor.matmul(st_ps[:, j, lo:S], kstk[0:KALL, h, key * P:(key + 1) * P],
                                               qstk[0:KALL, h, lo:S], start=True, stop=(b.steps == "B"))
                        if b.steps == "A":
                            ins = nc.tensor.matmul(st_ps[:, j, lo:lo + P], id_b[:, :], mask_k[:, :], start=False, stop=True)
                    ins.then_inc(st_full, 1)
                score_tile(b, tick, 2 * half)
                score_tile(b, tick, 2 * half + 1)

            def pv_step(b, tick):
                if (tick == 0 and not b.post) or (tick > 0 and not b.steps):
                    return
                unit, s, knd = (b.u - 1, TICKS - 1, b.post) if tick == 0 else (b.u, tick - 1, b.steps)
                g, key = s // T, s % T
                pe.wait_ge(exp_done, unit * 2 * TICKS + 2 * s + 2)
                if key == 0:
                    pe.wait_ge(vpad_ready, unit * NQ + g + 1)
                    if g % 2 == 0:
                        wait(pe, ev_done, unit * 2 + g // 2)
                lo = key * P if knd == "A" else 0
                for j in range(NJ):
                    ins = nc.tensor.matmul(pv_ps[32 * j:32 * j + 32, lo:S], vpad[:, key, g, j, :],
                                           probs[:, s % PBUF, j, lo:S], start=(key == 0 and g % 2 == 0),
                                           stop=(key == T - 1 and g % 2 == 1), tile_position=(0, 32 * j))
                ins.then_inc(pv_done, 1)

            def turn_off(b, v, g, name):
                pe.wait_ge(parts_ready, v * NQ + g + 1)
                wait(pe, misc_free, b.misc_use(name))
                for t in range(T):
                    ins = nc.tensor.transpose(misc_b[0:PARTS * NJ, t * P:(t + 1) * P],
                                              max_parts[:, g % 2, t, :, :].rearrange("p i j -> p (i j)"), id_b[:, :])
                ins.then_inc(misc_full, 1)

            def turn(b, name, src):
                wait(pe, misc_free, b.misc_use(name))
                for t in range(T):
                    ins = nc.tensor.transpose(misc[:, t * P:(t + 1) * P], src[:, t, :], id_f[:, :])
                ins.then_inc(misc_full, 1)

            def item(b, name):
                u = b.u
                w_qkv = w_a if b.prep == "A" else w_in
                if name == "off0":
                    turn_off(b, u + 1, 0, name)
                elif name in ("off1", "off2", "off3"):
                    turn_off(b, u, int(name[3]), name)
                elif name == "hT":
                    pe.wait_ge(h_ready, u + 2)
                    turn(b, name, h_sb)
                elif name in ("q", "k"):
                    if b.prep == "B" and name == "q":
                        pe.wait_ge(pb_in, (u + 2 - NA) * LOADS["pb"] * DMA)
                    wait(pe, misc_free, b.misc_use(name))
                    i = 0 if name == "q" else D
                    nc.tensor.matmul(misc[:, :], w_qkv[:, i:i + D], h_T[:, :], start=True, stop=True).then_inc(misc_full, 1)
                elif name == "v":
                    wait(pe, misc_free, b.misc_use(name))
                    for t in range(T):
                        ins = nc.tensor.matmul(misc[:, t * P:(t + 1) * P], h_T[:, t * P:(t + 1) * P], w_qkv[:, 2 * D:3 * D],
                                               start=True, stop=True)
                    ins.then_inc(misc_full, 1)
                elif name in ("O0", "O1"):
                    pe.wait_ge(ev_done, 2 * u)
                    wait(pe, misc_free, b.misc_use(name))
                    for i in range(2):
                        t = 2 * int(name[1]) + i
                        for gp in range(2):
                            ins = nc.tensor.transpose(misc[:, (2 * i + gp) * P:(2 * i + gp + 1) * P],
                                                      att_u[:, gp, t * P:(t + 1) * P], id_f[:, :])
                    ins.then_inc(misc_full, 1)
                elif name == "aT":
                    turn(b, name, attn)
                elif name in ("opA", "opB"):
                    w_o = w_a[:, 3 * D:4 * D] if name == "opA" else w_post[:, 0:D]
                    if name == "opB":
                        pe.wait_ge(qb_in, (u - NA) * LOADS["qb"] * DMA)
                    wait(pe, misc_free, b.misc_use(name))
                    for t in range(T):
                        ins = nc.tensor.matmul(misc[:, t * P:(t + 1) * P], attn_T[:, t * P:(t + 1) * P], w_o,
                                               start=True, stop=True)
                    ins.then_inc(misc_full, 1)
                elif name == "h2T":
                    pe.wait_ge(h2_ready, u)
                    turn(b, name, h2)
                elif name == "gate":
                    pe.wait_ge(hsum_ready, u)
                    wait(pe, misc_free, b.misc_use(name))
                    nc.tensor.matmul(misc[:, 0:NE], h_sum_b[:, :], gw[:, :], start=True, stop=True).then_inc(misc_full, 1)
                elif name == "x1T":
                    pe.wait_ge(x1_ready, u - NA)
                    turn(b, name, x1)
                elif name in ("ff0", "ff1", "ff2", "ff3"):
                    i = D + int(name[2]) * P
                    wait(pe, misc_free, b.misc_use(name))
                    nc.tensor.matmul(misc[:, :], w_post[:, i:i + P], x1_T[:, :], start=True, stop=True).then_inc(misc_full, 1)
                elif name == "out":
                    wait(pe, misc_free, b.misc_use(name))
                    for t in range(T):
                        for c in range(FC):
                            i = D + FF + c * D
                            ins = nc.tensor.matmul(misc[:, t * P:(t + 1) * P], hid[:, c, t * P:(t + 1) * P],
                                                   w_post[:, i:i + D], start=(c == 0), stop=(c == FC - 1))
                    ins.then_inc(misc_full, 1)

            walk(pe, half_step, item, pv_step)

        @block.vector
        def _(dve):
            v = nc.vector

            def over_tiles(row):
                return row.unsqueeze(1).to_broadcast([P, T, D])

            chain = Chain(dve, setup_chain, 21, 0)
            chain.link(v.memset(kstk[64:96, :, :], 1.0))
            chain.link(v.memset(vpad[:, :, :, :, :], 0.0))
            for g in range(NQ):
                i = (g % 2) * VW + HD
                chain.link(v.memset(vpad[:, :, g, :, i:i + 1], 1.0))
            for e in range(NE):
                chain.link(v.memset(before[:, e, :], 0.0))
                if e:
                    chain.link(v.memset(before[:, e, 0:e], 1.0))
                ins = v.memset(e_no[:, e:e + 1], float(e))
            ins.then_inc(ones_made, 1)
            dve.wait_ge(silu_exp, 1)
            chain.link(v.tensor_scalar(c_e[:, :], c_e[:, :], 1.0, None, ALU.add))
            chain.link(v.reciprocal(c_s[:, :], c_e[:, :]))
            v.tensor_tensor(c_s[:, :], c_s[:, :], c_T[:, :], ALU.mult).then_inc(silu_made, 1)
            dve.wait_ge(mod_mm, 2)
            for i in range(2):
                chain.link(v.tensor_copy(mod4[:, 3 * i:3 * i + 3, :].rearrange("b m d -> b (m d)"), s_ps[0:NB, i, 0:3 * D]))
            g_mod = mod4[:, 2:6:3, :]
            chain.link(v.tensor_scalar(mod_a[:, :, :], g_mod, -1.0, None, ALU.mult))
            chain.link(v.scalar_tensor_tensor(out=mod_a[:, :, :], in0=mod_a[:, :, :], scalar=0.25, in1=g_mod,
                                              op0=ALU.max, op1=ALU.max))
            chain.link(v.tensor_scalar(mod_s[:, :, :], g_mod, 0.0, 2.0, ALU.is_ge, ALU.mult))
            chain.link(v.tensor_scalar(mod_s[:, :, :], mod_s[:, :, :], -1.0, None, ALU.add))
            chain.end()
            v.tensor_tensor(g_mod, mod_s[:, :, :], mod_a[:, :, :], ALU.mult).then_inc(mod_made, 1)

            def ln_stats(chain, i, src):
                for t in range(T):
                    ins = v.bn_stats(stats[:, i, t, :], src[:, t, :])
                chain.link(ins, bare_next=True)
                for t in range(T):
                    ins = v.bn_aggr(mv[:, i, t, :], stats[:, i, t, :])
                chain.link(ins)
                v.tensor_scalar(var_e[:, i, :], mv[:, i, :, 1], EPS, None, ALU.add).then_inc(var_ready[i], 1)

            def ln_end(chain, i, unit, dst, src):
                dve.wait_ge(pow_ready[i], unit + 1)
                a, c = newton[:, i, 0, :], newton[:, i, 1, :]
                chain.link(v.tensor_tensor(a, rstd0[:, i, :], rstd0[:, i, :], ALU.mult))
                chain.link(v.tensor_tensor(c, a, var_e[:, i, :], ALU.mult))
                chain.link(v.tensor_scalar(a, c, -0.5, 1.5, ALU.mult, ALU.add))
                chain.link(v.tensor_tensor(rstd[:, i, :], a, rstd0[:, i, :], ALU.mult))
                for t in range(T):
                    ins = v.tensor_scalar(dst[:, t, :], src[:, t, :], mv[:, i, t, 0:1], rstd[:, i, t:t + 1],
                                          ALU.subtract, ALU.mult)
                chain.link(ins)

            def half_step(b, tick, half):
                knd, unit = (b.steps, b.u) if tick < 8 else (b.prep, b.u + 1)
                if not knd:
                    return
                g = 2 + tick // T if tick < 8 else (tick - 8) // T
                t = tick % T
                keys = (t + 1) * P if knd == "A" else S
                for c in (2 * half, 2 * half + 1):
                    n = b.u * NJ * TICKS + NJ * 8 + NJ * tick + c
                    dve.wait_ge(s_full, n + 1)
                    v.tensor_reduce(row_max[:, g % 2, t, c:c + 1], s_ps[:, c % 2, 0:keys], AX.X, ALU.max)\
                     .then_inc(max_done, 1)
                if t == T - 1 and half == 1:
                    q = g % 2
                    dve.wait_ge(max_done, n + 1)
                    chain = Chain(dve, parts_chain, 3, unit * NQ + g)
                    chain.link(v.tensor_scalar(max_parts[:, q, :, 0, :], row_max[:, q, :, :], -1.0, None, ALU.mult))
                    chain.link(v.scalar_tensor_tensor(out=max_r[:, q, :, :], in0=row_max[:, q, :, :], scalar=-1.0,
                                                      in1=max_parts[:, q, :, 0, :], op0=ALU.mult, op1=ALU.subtract))
                    chain.link(v.tensor_copy(max_parts[:, q, :, 1, :], max_r[:, q, :, :]))
                    chain.end()
                    v.tensor_tensor(max_parts[:, q, :, 2, :], max_r[:, q, :, :], max_parts[:, q, :, 1, :], ALU.subtract)\
                     .then_inc(parts_ready, 1)

            def pv_step(b, tick):
                pass

            open_chains = {}

            def item(b, name):
                u = b.u
                if name == "ln1a":
                    n = u + 1
                    dve.wait_ge(pa_in, (n + 1) * LOADS["pa"] * DMA)
                    open_chains["ln1"] = Chain(dve, ln1_chain, 9, n)
                    ln_stats(open_chains["ln1"], 0, x_in)
                    open_chains["ln1"].link(v.tensor_scalar(mod_c[:, :], mod_in[:, 1, :], 1.0, None, ALU.add))
                elif name == "ln1b":
                    c = open_chains["ln1"]
                    ln_end(c, 0, u + 1, h_sb, x_in)
                    c.link(v.tensor_tensor(h_sb[:, :, :], h_sb[:, :, :], over_tiles(mod_c[:, :]), ALU.mult))
                    c.end()
                    v.tensor_tensor(h_sb[:, :, :], h_sb[:, :, :], over_tiles(mod_in[:, 0, :]), ALU.add).then_inc(h_ready, 1)
                elif name == "q":
                    n = u + 1
                    dve.wait_ge(misc_free, b.misc_use("q") + 1)
                    wait(dve, scr_out, n * LOADS["scr"] * DMA)
                    c = Chain(dve, q_chain, 3, n)
                    c.link(v.tensor_copy(q_parts[:, 0, :], q_f[:, :]))
                    c.link(v.tensor_tensor(q_r[:, :], q_f[:, :], q_parts[:, 0, :], ALU.subtract))
                    c.link(v.tensor_copy(q_parts[:, 1, :], q_r[:, :]))
                    c.end()
                    v.tensor_tensor(q_parts[:, 2, :], q_r[:, :], q_parts[:, 1, :], ALU.subtract).then_inc(q_split, 1)
                elif name == "v":
                    bias = rows_a[:, 0, :] if b.prep == "A" else bv_in[:, :]
                    dve.wait_ge(misc_full, b.misc_use("v") + 1)
                    wait(dve, vpad_ready, (u + 1) * NQ)
                    v.tensor_tensor(v_sb[:, :, :], misc_t, over_tiles(bias), ALU.add).then_inc(misc_free, 1)
                elif name in ("O0", "O1"):
                    i = int(name[1])
                    src = misc[:, :].rearrange("p (h c) -> p h c", c=VW)
                    dve.wait_ge(misc_full, b.misc_use(name) + 1)
                    v.reciprocal(recip[:, i, :], src[:, :, HD]).then_inc(rec_done, 1)
                    dve.wait_ge(rec_done, (u - 1) * 2 + i + 1)
                    v.tensor_tensor(attn[:, 2 * i:2 * i + 2, :].rearrange("p t (h d) -> p (t h) d", d=HD), src[:, :, 0:HD],
                                    recip[:, i, :].unsqueeze(2).to_broadcast([P, 2 * NQ * NJ, HD]), ALU.mult)\
                     .then_inc(misc_free, 1)
                elif name == "opA":
                    n = u - 1
                    dve.wait_ge(misc_full, b.misc_use(name) + 1)
                    dve.wait_ge(qa_in, (n + 1) * LOADS["qa"] * DMA)
                    wait(dve, a_out, n * LOADS["a_out"] * DMA)
                    v.tensor_tensor(t1[:, :, :], misc_t, over_tiles(rows_a[:, 1, :]), ALU.add).then_inc(misc_free, 1)
                    dve.wait_ge(misc_free, b.misc_use(name) + 1)
                    c = open_chains["ln2"] = Chain(dve, ln2_chain, 11, n)
                    c.link(v.tensor_tensor(t1[:, :, :], t1[:, :, :], over_tiles(mod_post[:, 0, :]), ALU.mult))
                    c.link(v.tensor_tensor(x2[:, :, :], t1[:, :, :], x_post[:, :, :], ALU.add))
                    ln_stats(c, 1, x2)
                    c.link(v.tensor_scalar(mod_p1[:, :], mod_post[:, 2, :], 1.0, None, ALU.add))
                elif name == "ln2":
                    c = open_chains["ln2"]
                    ln_end(c, 1, u - 1, h2, x2)
                    c.link(v.tensor_tensor(h2[:, :, :], h2[:, :, :], over_tiles(mod_p1[:, :]), ALU.mult))
                    c.end()
                    v.tensor_tensor(h2[:, :, :], h2[:, :, :], over_tiles(mod_post[:, 1, :]), ALU.add).then_inc(h2_ready, 1)
                elif name == "gsum":
                    dve.wait_ge(misc_free, b.misc_use("h2T") + 1)
                    v.tensor_copy(h_sum_b[:, :], h_sum[:, :].to_broadcast([P, P])).then_inc(hsum_ready, 1)
                elif name == "gate":
                    n = u - 1
                    dve.wait_ge(misc_full, b.misc_use(name) + 1)
                    v.scalar_tensor_tensor(out=lg[:, :], in0=misc[:, 0:NE], scalar=1.0 / S, in1=gb_b[:, :],
                                           op0=ALU.mult, op1=ALU.add).then_inc(misc_free, 1)
                    dve.wait_ge(misc_free, b.misc_use(name) + 1)
                    c = Chain(dve, gate_chain, 11, n)
                    c.link(v.tensor_reduce(lmax[:, :], lg[:, :], AX.X, ALU.max))
                    v.tensor_scalar(lsh[:, :], lg[:, :], lmax[:, 0:1], None, ALU.subtract).then_inc(lsh_ready, 1)
                    other = lg[:, :].unsqueeze(1).to_broadcast([P, NE, NE])
                    own = lg[:, :].unsqueeze(2).to_broadcast([P, NE, NE])
                    v.tensor_tensor(gt[:, :, :], other, own, ALU.is_gt)
                    c.link(v.tensor_tensor(eq[:, :, :], other, own, ALU.is_equal))
                    c.link(v.tensor_tensor(eq[:, :, :], eq[:, :, :], before[:, :, :], ALU.mult))
                    c.link(v.tensor_tensor(gt[:, :, :], gt[:, :, :], eq[:, :, :], ALU.add))
                    c.link(v.tensor_reduce(rank[:, :], gt[:, :, :], AX.X, ALU.add))
                    for k in range(TOPK):
                        ins = v.tensor_scalar(pick[:, k, :], rank[:, :], float(k), None, ALU.is_equal)
                    c.link(ins)
                    c.link(v.tensor_tensor(pick_n[:, :, :], pick[:, :, :], e_no[:, :].unsqueeze(1).to_broadcast([P, TOPK, NE]), ALU.mult))
                    c.link(v.tensor_reduce(nsel_f[:, :], pick_n[:, :, :], AX.X, ALU.add))
                    v.tensor_copy(nsel[:, bass.ds(n * TOPK, TOPK)], nsel_f[:, :])
                    dve.wait_ge(lexp_ready, n + 1)
                    c.link(v.tensor_reduce(lsum[:, :], lexp[:, :], AX.X, ALU.add))
                    c.link(v.reciprocal(lrec[:, :], lsum[:, :]))
                    c.link(v.scalar_tensor_tensor(out=pick_w[:, :, :], in0=pick[:, :, :], scalar=lrec[:, 0:1],
                                                  in1=lexp[:, :].unsqueeze(1).to_broadcast([P, TOPK, NE]),
                                                  op0=ALU.mult, op1=ALU.mult))
                    c.end()
                    v.tensor_reduce(wsel[:, bass.ds(n * TOPK, TOPK)], pick_w[:, :, :], AX.X, ALU.add).then_inc(sel_ready, 1)
                elif name == "opB":
                    n = u - 1 - NA
                    dve.wait_ge(misc_full, b.misc_use(name) + 1)
                    v.tensor_tensor(t1[:, :, :], misc_t, over_tiles(rows_post[:, 0, :]), ALU.add).then_inc(misc_free, 1)
                    dve.wait_ge(misc_free, b.misc_use(name) + 1)
                    c = open_chains["ln3"] = Chain(dve, ln3_chain, 9, n)
                    c.link(v.tensor_tensor(t2[:, :, :], t1[:, :, :], h2_post[:, :, :], ALU.add))
                    ln_stats(c, 2, t2)
                elif name == "ln3":
                    c = open_chains["ln3"]
                    ln_end(c, 2, u - 1 - NA, x1, t2)
                    c.link(v.tensor_tensor(x1[:, :, :], x1[:, :, :], over_tiles(rows_post[:, 1, :]), ALU.mult))
                    c.end()
                    v.tensor_tensor(x1[:, :, :], x1[:, :, :], over_tiles(rows_post[:, 2, :]), ALU.add).then_inc(x1_ready, 1)
                elif name == "out":
                    n = u - 1 - NA
                    dve.wait_ge(misc_full, b.misc_use(name) + 1)
                    v.tensor_tensor(t1[:, :, :], misc_t, over_tiles(rows_post[:, 3, :]), ALU.add).then_inc(misc_free, 1)
                    dve.wait_ge(misc_free, b.misc_use(name) + 1)
                    c = open_chains["ln4"] = Chain(dve, ln4_chain, 11, n)
                    c.link(v.tensor_tensor(t2[:, :, :], t1[:, :, :], x1[:, :, :], ALU.add))
                    ln_stats(c, 3, t2)
                elif name == "ln4":
                    n = u - 1 - NA
                    c = open_chains["ln4"]
                    v.tensor_copy(gate_q[:, :], wsel[:, bass.ds(n, 1)])
                    ln_end(c, 3, n, y, t2)
                    c.link(v.tensor_tensor(y[:, :, :], y[:, :, :], over_tiles(rows_post[:, 4, :]), ALU.mult))
                    c.link(v.tensor_tensor(y[:, :, :], y[:, :, :], over_tiles(rows_post[:, 5, :]), ALU.add))
                    c.link(v.scalar_tensor_tensor(out=y[:, :, :], in0=y[:, :, :], scalar=gate_q[:, 0:1],
                                                  in1=over_tiles(gb_post[:, :]), op0=ALU.mult, op1=ALU.mult))
                    c.end()
                    v.tensor_tensor(acc[:, :, :], y[:, :, :], x_post[:, :, :], ALU.add).then_inc(acc_ready, 1)

            walk(dve, half_step, item, pv_step)


def kernel(**inputs):
    import numpy as _np
    import concourse.bacc as _bacc
    from concourse import mybir as _mybir
    from concourse.bass_utils import run_bass_kernel_spmd as _run

    a = {k: _np.asarray(v) for k, v in inputs.items()}
    at = {k[len("L0_attn_"):]: v for k, v in a.items() if k.startswith("L0_attn_")}
    ff = {k[len("L0_ffn_"):]: v for k, v in a.items() if k.startswith("L0_ffn_")}
    ne = ff["gate_w"].shape[0]
    turned = lambda w: w.transpose(0, 2, 1)
    lin2 = turned(ff["lin2_w"]).reshape(ne, FC, P, D).transpose(0, 2, 1, 3).reshape(ne, P, FC * D)
    cat = _np.concatenate
    arrays = {
        "x": at["x"],
        "w_attn": cat([at["Wq"], at["Wk"], at["Wv"], at["Wmix"]], axis=1),
        "cols_attn": _np.stack([at["bq"], at["bk"]], axis=1),
        "rows_attn": _np.stack([at["bv"], at["bmix"]]),
        "w_exp": cat([turned(ff["in_proj_w"]), turned(ff["in_proj_b"][:, 0:2 * D].reshape(ne, 2, D)),
                      turned(ff["out_proj_w"]), turned(ff["lin1_w"]), lin2,
                      turned(ff["lin1_b"].reshape(ne, FC, P))], axis=2),
        "rows_exp": cat([ff["in_proj_b"][:, 2 * D:3 * D], ff["out_proj_b"], ff["ln1_w"], ff["ln1_b"], ff["lin2_b"],
                         ff["ln2_w"], ff["ln2_b"]], axis=1),
        "gate_wT": ff["gate_w"].T,
        "gate_b": ff["gate_b"],
        "cT": a["L0_c"].T,
        "wmod": a["L0_wmod"],
    }
    arrays = {f"in_{k}": _np.ascontiguousarray(v) for k, v in arrays.items()}
    nc = _bacc.Bacc("TRN2", target_bir_lowering=False, num_devices=1)
    args = [nc.dram_tensor(k, v.shape, _mybir.dt.from_np(v.dtype), kind="ExternalInput").ap() for k, v in arrays.items()]
    args.append(nc.dram_tensor("out_x", arrays["in_x"].shape, _mybir.dt.float32, kind="ExternalOutput").ap())
    adaln_kernel(nc, *args)
    r = _run(nc, [arrays], core_ids=[0])
    return r.results[0]["out_x"]
```

```python
from contextlib import ExitStack

import concourse.bass as bass
from concourse import mybir

F32 = mybir.dt.float32
BF16 = mybir.dt.bfloat16
I32 = mybir.dt.int32
ALU = mybir.AluOpType
ACT = mybir.ActivationFunctionType
AX = mybir.AxisListType

P = 128
NB, S, D = 4, 512, 128
HD = 8
T = S // P
NE, TOPK, FF = 4, 2, 512
FC = FF // P
NQ = 4
NJ = 4
PARTS = 3
KROWS = PARTS * PARTS * HD
KALL = KROWS + PARTS
VW = 16
TICKS = NQ * T
PBUF = 4
EPS = 1e-5
SCALE = HD ** -0.5
MASKED = -1e30
NA = NB
NU = NA + NB * TOPK
W_IN, W_POST = 3 * D + 2, D + FF + FC * D + FC + 3
DMA = 16


def kind(u):
    return "A" if u < NA else "B"


ATTN_ITEMS = [(0, 0, "off1"), (0, 0, "stk3"), (1, 0, "vp3"), (4, 0, "off2"), (8, 0, "off3")]
PREP_ITEMS = {
    "A": [(0, 0, "loadA"), (0, 1, "ln1a"), (1, 0, "ln1b"), (1, 1, "hT"), (2, 1, "q"), (3, 0, "q2"), (3, 1, "k"),
          (4, 0, "k2"), (4, 1, "v"), (4, 1, "scr")],
    "B": [(0, 0, "loadB"), (1, 1, "q"), (2, 0, "q2"), (2, 1, "k"), (3, 0, "k2"), (3, 0, "scr"), (3, 1, "v")],
    "all": [(5, 0, "stk0"), (5, 1, "vp0"), (8, 0, "stk1"), (9, 0, "vp1"), (12, 0, "stk2"), (12, 0, "off0"),
            (13, 0, "vp2")],
}
POST_ITEMS = {
    "A": [(0, 0, "loadPA"), (1, 0, "O0"), (2, 0, "O1"), (2, 1, "preA"), (3, 0, "aT"), (5, 1, "opA"), (6, 0, "ln2"),
          (6, 1, "h2T"), (7, 0, "gsum"), (7, 1, "gate")],
    "B": [(0, 0, "loadPB"), (1, 0, "O0"), (2, 0, "O1"), (2, 1, "preB"), (3, 0, "aT"), (4, 1, "opB"), (5, 0, "ln3"),
          (5, 1, "x1T"), (6, 1, "ff0"), (7, 1, "ff1"), (8, 1, "ff2"), (9, 1, "ff3"), (10, 1, "out"),
          (11, 1, "ln4")],
}
MISC = ("off0", "off1", "off2", "off3", "hT", "q", "k", "v", "O0", "O1", "aT", "opA", "opB", "h2T",
        "gate", "x1T", "ff0", "ff1", "ff2", "ff3", "out")


class Body:

    def __init__(self, first, count, misc_base):
        self.first, self.count, self.misc_base = first, count, misc_base
        u = first
        self.steps = kind(u) if 0 <= u < NU else None
        self.prep = kind(u + 1) if u + 1 < NU else None
        self.post = kind(u - 1) if 0 <= u - 1 < NU else None
        items = []
        if self.prep:
            items += PREP_ITEMS[self.prep] + PREP_ITEMS["all"]
        if self.steps:
            items += ATTN_ITEMS
        if self.post:
            items += POST_ITEMS[self.post]
        self.items = sorted(items, key=lambda i: (i[0], i[1]))
        self.misc = [n for _, _, n in self.items if n in MISC]

    def at(self, u):
        self.u = u
        self.misc_now = self.misc_base + (u - self.first) * len(self.misc)
        return self

    def misc_use(self, name):
        return self.misc_now + self.misc.index(name)


def bodies():
    out, base = [], 0
    for first, count in ((-1, 1), (0, 1), (1, 1), (2, 1), (3, 1), (4, 1), (5, 1), (6, NU - 7), (NU - 1, 1), (NU, 1)):
        out.append(Body(first, count, base))
        base += count * len(out[-1].misc)
    return out


def walk(eng, half_step, item, pv_step):
    def emit(b):
        for tick in range(TICKS):
            for half in range(2):
                half_step(b, tick, half)
                if half == 0:
                    pv_step(b, tick)
                for t, h, name in b.items:
                    if (t, h) == (tick, half):
                        item(b, name)

    for b in bodies():
        if b.count == 1:
            emit(b.at(b.first))
        else:
            with eng.Fori(b.first, b.first + b.count) as u:
                emit(b.at(u))


def adaln_kernel(nc, x, w_attn, cols_attn, row_attn, w_exp, rows_exp, gate_wT, gate_b, cT, wmod, out):
    ctx = ExitStack()
    with ctx:
        def sb(name, shape, dt=F32):
            return ctx.enter_context(nc.sbuf_tensor(name, shape, dt))

        def pb(name, shape, dt=F32):
            return ctx.enter_context(nc.psum_tensor(name, shape, dt))

        def sem(name):
            return ctx.enter_context(nc.semaphore(name))

        kstk = sb("kstk", [P, NQ * NJ, S], BF16)
        qstk = sb("qstk", [P, NQ * NJ, S], BF16)
        probs = sb("probs", [P, PBUF, NJ, S])
        vpad = sb("vpad", [P, T, NQ, NJ, 2 * VW])
        v_sb = sb("v_sb", [P, T, D])
        att_u = sb("att_u", [P, 2, S])
        x_n = sb("x_n", [P, T, D])
        h_T = sb("h_T", [P, S])
        q_f = sb("q_f", [P, S])
        k_f = sb("k_f", [P, S])
        q_r = sb("q_r", [P, S])
        k_r = sb("k_r", [P, S])
        q_parts = sb("q_parts", [P, PARTS, S], BF16)
        k_parts = sb("k_parts", [P, PARTS, S], BF16)
        row_max = sb("row_max", [P, 2, T, NJ])
        max_r = sb("max_r", [P, 2, T, NJ])
        max_parts = sb("max_parts", [P, 2, T, PARTS, NJ], BF16)
        off_rows = sb("off_rows", [PARTS * NJ, 2, S], BF16)
        w_a = sb("w_a", [P, 4 * D])
        cols_a = sb("cols_a", [P, 3])
        row_a = sb("row_a", [P, D])
        w_in = sb("w_in", [P, W_IN])
        w_post = sb("w_post", [P, W_POST])
        rows_post = sb("rows_post", [P, 6, D])
        x_in = sb("x_in", [P, T, D])
        x_post = sb("x_post", [P, T, D])
        mod_post = sb("mod_post", [P, 3, D])
        mod_p1 = sb("mod_p1", [P, D])
        gb_post = sb("gb_post", [P, D])
        h2_post = sb("h2_post", [P, T, D])
        recip = sb("recip", [P, 2, 2 * NQ * NJ])
        attn = sb("attn", [P, T, D])
        attn_T = sb("attn_T", [P, S])
        t1 = sb("t1", [P, T, D])
        x_pre = sb("x_pre", [P, T, D])
        row_t = sb("row_t", [P, D])
        row_w = sb("row_w", [P, D])
        row_g = sb("row_g", [P, D])
        h2_n = sb("h2_n", [P, T, D])
        x1_n = sb("x1_n", [P, T, D])
        y_n = sb("y_n", [P, T, D])
        out_pre = sb("out_pre", [P, T, D])
        t2 = sb("t2", [P, T, D])
        x2 = sb("x2", [P, T, D])
        h2 = sb("h2", [P, T, D])
        h2_T = sb("h2_T", [P, S])
        x1 = sb("x1", [P, T, D])
        x1_T = sb("x1_T", [P, S])
        hid = sb("hid", [P, FC, S])
        y = sb("y", [P, T, D])
        acc = sb("acc", [P, T, D])
        stats = sb("stats", [P, 4, T, 6])
        mv = sb("mv", [P, 4, T, 2])
        var_e = sb("var_e", [P, 4, T])
        rstd0 = sb("rstd0", [P, 4, T])
        newton = sb("newton", [P, 4, 2, T])
        minus_half = sb("minus_half", [P, T])
        rstd = sb("rstd", [P, 4, T])
        shift = sb("shift", [P, 4, T])
        h_sum = sb("h_sum", [P, 1])
        h_sum_b = sb("h_sum_b", [P, P])
        gw = sb("gw", [P, NE])
        gb_b = sb("gb_b", [P, NE])
        before = sb("before", [P, NE, NE])
        e_no = sb("e_no", [P, NE])
        lg = sb("lg", [P, NE])
        lmax = sb("lmax", [P, 1])
        lsh = sb("lsh", [P, NE])
        lexp = sb("lexp", [P, NE])
        lsum = sb("lsum", [P, 1])
        lrec = sb("lrec", [P, 1])
        gt = sb("gt", [P, NE, NE])
        eq = sb("eq", [P, NE, NE])
        rank = sb("rank", [P, NE])
        pick = sb("pick", [P, TOPK, NE])
        pick_w = sb("pick_w", [P, TOPK, NE])
        pick_n = sb("pick_n", [P, TOPK, NE])
        nsel_f = sb("nsel_f", [P, TOPK])
        wsel = sb("wsel", [P, NB * TOPK])
        nsel = sb("nsel", [P, NB * TOPK], I32)
        c_T = sb("c_T", [P, NB])
        c_e = sb("c_e", [P, NB])
        c_s = sb("c_s", [P, NB])
        w_mod = sb("w_mod", [P, 6 * D])
        mod4 = sb("mod4", [NB, 6, D])
        mod_a = sb("mod_a", [NB, 2, D])
        mod_s = sb("mod_s", [NB, 2, D])
        mod_cols = sb("mod_cols", [P, 6, NB])
        zeros = sb("zeros", [P, P])
        ones_row = sb("ones_row", [P, D])
        id_f = sb("id_f", [P, P])
        id_b = sb("id_b", [P, P], BF16)
        mask_q = sb("mask_q", [P, P], BF16)
        mask_k = sb("mask_k", [P, P], BF16)
        neg = sb("neg", [P, P], BF16)

        st_ps = pb("st_ps", [P, 4, S])
        s_ps = pb("s_ps", [P, 2, S])
        pv_ps = pb("pv_ps", [P, S])
        misc = pb("misc", [P, S])
        misc_b = misc[:, :].bitcast(BF16)
        misc_t = misc[:, :].rearrange("p (t d) -> p t d", t=T)

        stk_shape = [NQ * NJ, PARTS, PARTS, HD, S]
        q_dram = nc.dram_tensor("q_scratch", stk_shape, BF16).ap()
        k_dram = nc.dram_tensor("k_scratch", stk_shape, BF16).ap()
        mod_dram = nc.dram_tensor("mod_scratch", [NB, 6 * D], F32).ap()
        h2_dram = nc.dram_tensor("h2_scratch", [NB, S, D], F32).ap()
        h2T_dram = nc.dram_tensor("h2T_scratch", [NB, P, S], F32).ap()

        def tokens(a):
            return a.rearrange("(t p) d -> p t d", p=P)

        q_rows = q_dram.rearrange("(gp j sub) a i d n -> gp sub (a i d) j n", gp=2, j=NJ)
        k_rows = k_dram.rearrange("(gp j sub) a i d n -> gp sub (a i d) j n", gp=2, j=NJ)

        consts_in = sem("consts_in")
        cmod_in = sem("cmod_in")
        consts_made = sem("consts_made")
        ones_made = sem("ones_made")
        setup_chain = sem("setup_chain")
        setup_pool = sem("setup_pool")
        silu_exp = sem("silu_exp")
        silu_made = sem("silu_made")
        mod_mm = sem("mod_mm")
        mod_made = sem("mod_made")
        mod_out = sem("mod_out")
        st_full = sem("st_full")
        exp_done = sem("exp_done")
        s_full = sem("s_full")
        max_done = sem("max_done")
        parts_ready = sem("parts_ready")
        parts_chain = sem("parts_chain")
        off_in = [sem(f"off{g}_in") for g in range(NQ)]
        pv_done = sem("pv_done")
        ev_done = sem("ev_done")
        misc_full = sem("misc_full")
        misc_free = sem("misc_free")
        ln1_chain = sem("ln1_chain")
        ln2_chain = sem("ln2_chain")
        ln3_chain = sem("ln3_chain")
        ln4_chain = sem("ln4_chain")
        var_ready = [sem(f"var{i}_ready") for i in range(4)]
        pow_ready = [sem(f"pow{i}_ready") for i in range(4)]
        rstd_ready = [sem(f"rstd{i}_ready") for i in range(4)]
        norm_ready = [sem(f"norm{i}_ready") for i in range(4)]
        rest_ready = {n: sem(f"{n}_rest_ready") for n in "qk"}
        part_ready = {n: sem(f"{n}_part_ready") for n in "qk"}
        split = {n: sem(f"{n}_split") for n in "qk"}
        scr_out = sem("scr_out")
        stk_in = [sem(f"stk{g}_in") for g in range(NQ)]
        vpad_ready = sem("vpad_ready")
        pa_in = sem("pa_in")
        pb_in = sem("pb_in")
        qa_in = sem("qa_in")
        qb_in = sem("qb_in")
        rec_done = sem("rec_done")
        x2_ready = sem("x2_ready")
        h2_ready = sem("h2_ready")
        hsum_ready = sem("hsum_ready")
        pre_ready = {k: sem(f"pre{k}_ready") for k in "AB"}
        pre_chain = sem("pre_chain")
        h2_chain = sem("h2_chain")
        x1_chain = sem("x1_chain")
        y_chain = sem("y_chain")
        gate_chain = sem("gate_chain")
        lsh_ready = sem("lsh_ready")
        lexp_ready = sem("lexp_ready")
        sel_ready = sem("sel_ready")
        a_out = sem("a_out")
        x1_ready = sem("x1_ready")
        acc_ready = sem("acc_ready")
        b_out = sem("b_out")

        LOADS = {"pa": 1, "pb": 2, "qa": 2, "qb": 5, "a_out": 3, "const": 5, "scr": 2 * PARTS * PARTS}

        block = ctx.enter_context(nc.Block())

        def wait(eng, s, value, bare=False):
            if isinstance(value, int):
                if value > 0:
                    eng.wait_ge(s, value)
                return
            if bare or eng.engine == nc.sync.engine:
                value = eng.to_reg(value)
                true_since_setup, n = {nc.sync.engine: (mod_out, DMA), nc.gpsimd.engine: (consts_made, 1),
                                       nc.vector.engine: (ones_made, 1)}[eng.engine]
                eng.wait_ge(true_since_setup, n)
            eng.wait_ge(s, value)

        def over_tiles(row):
            return row.unsqueeze(1).to_broadcast([P, T, D])

        class Chain:

            def __init__(self, eng, s, per, unit):
                self.eng, self.s, self.per, self.base, self.n = eng, s, per, unit * per, 0

            def link(self, ins, bare_next=False):
                self.n += 1
                ins.then_inc(self.s, 1)
                wait(self.eng, self.s, self.base + self.n, bare_next)

            def end(self):
                assert self.n == self.per, (self.n, self.per)

        @block.sync
        def _(sp):
            sp.dma_start(c_T[:, :], cT).then_inc(cmod_in, DMA)
            sp.dma_start(w_mod[:, :], wmod).then_inc(cmod_in, DMA)
            sp.dma_start(w_a[:, :], w_attn).then_inc(consts_in, DMA)
            sp.dma_start(cols_a[:, :], cols_attn).then_inc(consts_in, DMA)
            sp.dma_start(row_a[:, :], row_attn.partition_broadcast(P)).then_inc(consts_in, DMA)
            sp.dma_start(gw[:, :], gate_wT).then_inc(consts_in, DMA)
            sp.dma_start(gb_b[:, :], gate_b.partition_broadcast(P)).then_inc(consts_in, DMA)
            sp.wait_ge(mod_made, 1)
            sp.dma_start(mod_dram, mod4[:, :, :].rearrange("b m d -> b (m d)")).then_inc(mod_out, DMA)
            sp.wait_ge(mod_out, DMA)

            def half_step(b, tick, half):
                pass

            def pv_step(b, tick):
                pass

            def load_stack(v, g):
                wait(sp, st_full, (v - 1) * 2 * TICKS + 2 * T * (g + 1))
                wait(sp, s_full, (v - 1) * NJ * TICKS + NJ * T * (g + 1))
                for dst, src in ((qstk, q_rows), (kstk, k_rows)):
                    sp.dma_start(dst[0:KROWS, NJ * g:NJ * g + NJ, :], src[g // 2, g % 2]).then_inc(stk_in[g], DMA)

            def load_off(b, v, g, name):
                wait(sp, misc_free, b.misc_use(name) + 1)
                sp.dma_start(qstk[KROWS:KALL, NJ * g:NJ * g + NJ, :], off_rows[:, g % 2, :]).then_inc(off_in[g], DMA)

            def item(b, name):
                u = b.u
                if name == "stk3":
                    load_stack(u, 3)
                elif name in ("stk0", "stk1", "stk2"):
                    load_stack(u + 1, int(name[3]))
                elif name == "off0":
                    load_off(b, u + 1, 0, name)
                elif name in ("off1", "off2", "off3"):
                    load_off(b, u, int(name[3]), name)
                elif name == "loadA":
                    v = u + 1
                    wait(sp, norm_ready[0], v)
                    sp.dma_start(x_in[:, :, :], tokens(x[v])).then_inc(pa_in, DMA)
                elif name == "loadB":
                    w = u + 1 - NA
                    wait(sp, sel_ready, w // TOPK + 1)
                    wait(sp, a_out, (w // TOPK + 1) * LOADS["a_out"] * DMA)
                    e = sp.value_load(nsel[0:1, bass.ds(w, 1)], min_val=0, max_val=NE - 1)
                    wait(sp, vpad_ready, (w + NA) * NQ - 1)
                    sp.dma_start(h_T[:, :], h2T_dram[w // TOPK]).then_inc(pb_in, DMA)
                    sp.dma_start(w_in[:, :], w_exp[e, :, 0:W_IN]).then_inc(pb_in, DMA)
                elif name == "scr":
                    v = u + 1
                    for g in range(NQ):
                        wait(sp, stk_in[g], v * 2 * DMA)
                    wait(sp, split["q"], v + 1)
                    for i in range(PARTS):
                        for a in range(PARTS):
                            sp.dma_start(q_dram[:, a, i], q_parts[:, i, :]).then_inc(scr_out, DMA)
                    wait(sp, split["k"], v + 1)
                    for a in range(PARTS):
                        for i in range(PARTS):
                            sp.dma_start(k_dram[:, a, i], k_parts[:, a, :]).then_inc(scr_out, DMA)
                    wait(sp, scr_out, (v + 1) * LOADS["scr"] * DMA)
                elif name == "loadPA":
                    v = u - 1
                    wait(sp, h2_ready, v)
                    sp.dma_start(x_post[:, :, :], tokens(x[v])).then_inc(qa_in, DMA)
                    sp.dma_start(mod_post[:, :, :].rearrange("p m d -> p (m d)"),
                                 mod_dram[v, 2 * D:5 * D].partition_broadcast(P)).then_inc(qa_in, DMA)
                elif name == "loadPB":
                    w = u - 1 - NA
                    if isinstance(w, int) and w == 0:
                        wait(sp, a_out, NA * LOADS["a_out"] * DMA)
                    else:
                        wait(sp, b_out, w * DMA)
                    e = sp.value_load(nsel[0:1, bass.ds(w, 1)], min_val=0, max_val=NE - 1)
                    sp.dma_start(w_post[:, :], w_exp[e, :, W_IN:W_IN + W_POST]).then_inc(qb_in, DMA)
                    sp.dma_start(rows_post[:, :, :].rearrange("p m d -> p (m d)"),
                                 rows_exp[e].partition_broadcast(P)).then_inc(qb_in, DMA)
                    sp.dma_start(gb_post[:, :], mod_dram[w // TOPK, 5 * D:6 * D].partition_broadcast(P)).then_inc(qb_in, DMA)
                    sp.dma_start(h2_post[:, :, :], tokens(h2_dram[w // TOPK])).then_inc(qb_in, DMA)
                    sp.dma_start(x_post[:, :, :], tokens(out[w // TOPK])).then_inc(qb_in, DMA)
                elif name == "h2T":
                    v = u - 1
                    wait(sp, x2_ready, v + 1)
                    sp.dma_start(tokens(out[v]), x2[:, :, :]).then_inc(a_out, DMA)
                    wait(sp, misc_free, b.misc_use(name) + 1)
                    sp.dma_start(h2T_dram[v], h2_T[:, :]).then_inc(a_out, DMA)
                    wait(sp, h2_ready, v + 1)
                    sp.dma_start(tokens(h2_dram[v]), h2[:, :, :]).then_inc(a_out, DMA)
                elif name == "ln4":
                    w = u - 1 - NA
                    wait(sp, acc_ready, w + 1)
                    sp.dma_start(tokens(out[w // TOPK]), acc[:, :, :]).then_inc(b_out, DMA)

            walk(sp, half_step, item, pv_step)
            sp.wait_ge(b_out, NB * TOPK * DMA)

        @block.gpsimd
        def _(pool):
            chain = Chain(pool, setup_pool, 7, 0)
            nc.gpsimd.memset(ones_row[:, :], 1.0)
            chain.link(nc.gpsimd.memset(id_f[:, :], 0.0))
            chain.link(nc.gpsimd.memset(zeros[:, :], 0.0))
            chain.link(nc.gpsimd.affine_select(out=id_f[:, :], in_=id_f[:, :], compare_op=ALU.not_equal, fill=1.0,
                                               base=0, pattern=[[-1, P]], channel_multiplier=1))
            chain.link(nc.gpsimd.tensor_copy(id_b[:, :], id_f[:, :]))
            chain.link(nc.gpsimd.affine_select(out=neg[:, :], in_=zeros[:, :], compare_op=ALU.is_ge, fill=MASKED,
                                               base=0, pattern=[[-1, P]], channel_multiplier=1))
            chain.link(nc.gpsimd.tensor_copy(mask_q[:, :], neg[:, :]))
            chain.link(nc.gpsimd.affine_select(out=mask_k[:, :], in_=zeros[:, :], compare_op=ALU.is_ge, fill=MASKED,
                                               base=0, pattern=[[1, P]], channel_multiplier=-1))
            chain.end()
            nc.gpsimd.memset(minus_half[:, :], -0.5).then_inc(consts_made, 1)
            pool.wait_ge(consts_made, 1)

            def half_step(b, tick, half):
                pass

            def pv_step(b, tick):
                pass

            pool_tt = nc.gpsimd.tensor_tensor

            def power(i, unit):
                pool.wait_ge(var_ready[i], unit + 1)
                nc.gpsimd.tensor_tensor(rstd0[:, i, :], var_e[:, i, :], minus_half[:, :], ALU.pow)\
                  .then_inc(pow_ready[i], 1)

            def place_v(v, g):
                gp, sub = g // 2, g % 2
                wait(pool, pv_done, (v - 1) * TICKS + T * (g + 1), bare=True)
                nc.gpsimd.tensor_copy(
                    vpad[:, :, g, :, sub * VW:sub * VW + HD],
                    v_sb[:, :, :].rearrange("p k (gp j sub d) -> p k gp j sub d", gp=2, j=NJ, sub=2)[:, :, gp, :, sub, :],
                ).then_inc(vpad_ready, 1)

            def item(b, name):
                u = b.u
                if name == "ln1a":
                    power(0, u + 1)
                elif name == "opA":
                    power(1, u - 1)
                elif name == "opB":
                    power(2, u - 1 - NA)
                elif name == "out":
                    power(3, u - 1 - NA)
                elif name in ("q", "k"):
                    full, rest, parts = (q_f, q_r, q_parts) if name == "q" else (k_f, k_r, k_parts)
                    wait(pool, misc_free, b.misc_use(name) + 1)
                    pool_tt(rest[:, :], full[:, :], parts[:, 0, :], ALU.subtract).then_inc(rest_ready[name], 1)
                elif name in ("q2", "k2"):
                    rest, parts = (q_r, q_parts) if name == "q2" else (k_r, k_parts)
                    wait(pool, part_ready[name[0]], u + 2)
                    pool_tt(parts[:, 2, :], rest[:, :], parts[:, 1, :], ALU.subtract).then_inc(split[name[0]], 1)
                elif name == "preA":
                    pool.wait_ge(qa_in, u * LOADS["qa"] * DMA)
                    c = Chain(pool, pre_chain, 1, u - 1)
                    c.link(pool_tt(row_t[:, :], row_a[:, :], mod_post[:, 0, :], ALU.mult))
                    pool_tt(x_pre[:, :, :], x_post[:, :, :], over_tiles(row_t[:, :]), ALU.add).then_inc(pre_ready["A"], 1)
                elif name == "ln2":
                    n = u - 1
                    wait(pool, a_out, n * LOADS["a_out"] * DMA)
                    c = Chain(pool, h2_chain, 2, n)
                    c.link(pool_tt(row_w[:, :], mod_post[:, 2, :], ones_row[:, :], ALU.add))
                    wait(pool, norm_ready[1], n + 1)
                    c.link(pool_tt(h2[:, :, :], h2_n[:, :, :], over_tiles(row_w[:, :]), ALU.mult))
                    c.end()
                    pool_tt(h2[:, :, :], h2[:, :, :], over_tiles(mod_post[:, 1, :]), ALU.add).then_inc(h2_ready, 1)
                elif name == "preB":
                    pool.wait_ge(qb_in, (u - NA) * LOADS["qb"] * DMA)
                    pool_tt(x_pre[:, :, :], h2_post[:, :, :], over_tiles(rows_post[:, 0, :]), ALU.add)\
                        .then_inc(pre_ready["B"], 1)
                elif name == "ln3":
                    n = u - 1 - NA
                    pool_tt(row_t[:, :], rows_post[:, 2, :], rows_post[:, 3, :], ALU.add)
                    wait(pool, norm_ready[2], n + 1)
                    c = Chain(pool, x1_chain, 1, n)
                    c.link(pool_tt(x1[:, :, :], x1_n[:, :, :], over_tiles(rows_post[:, 1, :]), ALU.mult))
                    c.end()
                    pool_tt(x1[:, :, :], x1[:, :, :], over_tiles(row_t[:, :]), ALU.add).then_inc(x1_ready, 1)
                elif name == "ln4":
                    n = u - 1 - NA
                    c = Chain(pool, y_chain, 4, n)
                    c.link(pool_tt(row_g[:, :], gb_post[:, :], wsel[:, bass.ds(n, 1)].to_broadcast([P, D]), ALU.mult))
                    pool_tt(row_w[:, :], rows_post[:, 4, :], row_g[:, :], ALU.mult)
                    c.link(pool_tt(row_t[:, :], rows_post[:, 5, :], row_g[:, :], ALU.mult))
                    c.link(pool_tt(out_pre[:, :, :], x_post[:, :, :], over_tiles(row_t[:, :]), ALU.add))
                    wait(pool, norm_ready[3], n + 1)
                    c.link(pool_tt(y[:, :, :], y_n[:, :, :], over_tiles(row_w[:, :]), ALU.mult))
                    c.end()
                    pool_tt(acc[:, :, :], y[:, :, :], out_pre[:, :, :], ALU.add).then_inc(acc_ready, 1)
                elif name == "vp3":
                    place_v(u, 3)
                elif name in ("vp0", "vp1", "vp2"):
                    if name == "vp0":
                        wait(pool, misc_free, b.misc_use("v") + 1, bare=True)
                        wait(pool, ones_made, 1)
                    place_v(u + 1, int(name[2]))

            walk(pool, half_step, item, pv_step)

        @block.scalar
        def _(act):
            act.wait_ge(cmod_in, 2 * DMA)
            nc.scalar.activation(c_e[:, :], c_T[:, :], ACT.Exp, scale=-1.0).then_inc(silu_exp, 1)

            def half_step(b, tick, half):
                if not b.steps:
                    return
                n = b.u * 2 * TICKS + 2 * tick + half
                key = tick % T
                lo = key * P if b.steps == "A" else 0
                act.wait_ge(st_full, n + 1)
                wait(act, pv_done, b.u * TICKS + tick - (PBUF - 1))
                nc.scalar.activation(probs[:, tick % PBUF, 2 * half:2 * half + 2, lo:S],
                                     st_ps[:, 2 * half:2 * half + 2, lo:S], ACT.Exp, scale=SCALE)\
                  .then_inc(exp_done, 1)

            def pv_step(b, tick):
                gp = {8: 0, 0: 1}.get(tick)
                if gp is None or (gp == 0 and not b.steps) or (gp == 1 and not b.post):
                    return
                unit = b.u if gp == 0 else b.u - 1
                act.wait_ge(pv_done, unit * TICKS + 8 * (gp + 1))
                nc.scalar.activation(att_u[:, gp, :], pv_ps[:, :], ACT.Copy).then_inc(ev_done, 1)

            def normalise(i, unit, dst, src):
                act.wait_ge(rstd_ready[i], unit + 1)
                for t in range(T):
                    ins = nc.scalar.activation(dst[:, t, :], src[:, t, :], ACT.Identity, bias=shift[:, i, t:t + 1],
                                               scale=rstd[:, i, t:t + 1])
                ins.then_inc(norm_ready[i], 1)

            def copy_off(b, v, g, name):
                act.wait_ge(misc_full, b.misc_use(name) + 1)
                wait(act, off_in[(g - 2) % NQ], (v + (g >= 2)) * DMA)
                nc.scalar.activation(off_rows[:, g % 2, :], misc_b[0:PARTS * NJ, 0:S], ACT.Copy).then_inc(misc_free, 1)

            def item(b, name):
                u = b.u
                if name == "off0":
                    copy_off(b, u + 1, 0, name)
                elif name in ("off1", "off2", "off3"):
                    copy_off(b, u, int(name[3]), name)
                elif name == "ln1b":
                    normalise(0, u + 1, x_n, x_in)
                elif name == "ln2":
                    wait(act, h2_ready, u - 1)
                    normalise(1, u - 1, h2_n, x2)
                elif name == "ln3":
                    wait(act, x1_ready, u - 1 - NA)
                    normalise(2, u - 1 - NA, x1_n, t2)
                elif name == "ln4":
                    wait(act, acc_ready, u - 1 - NA)
                    normalise(3, u - 1 - NA, y_n, t2)
                elif name == "hT":
                    act.wait_ge(misc_full, b.misc_use(name) + 1)
                    ca, sa = mod_cols[:, 1, bass.ds(u + 1, 1)], mod_cols[:, 0, bass.ds(u + 1, 1)]
                    nc.scalar.activation(h_T[:, :], misc[:, :], ACT.Identity, bias=sa, scale=ca).then_inc(misc_free, 1)
                elif name in ("q", "k"):
                    act.wait_ge(misc_full, b.misc_use(name) + 1)
                    col = 0 if name == "q" else 1
                    bias = cols_a[:, col:col + 1] if b.prep == "A" else w_in[:, 3 * D + col:3 * D + col + 1]
                    full, parts = (q_f, q_parts) if name == "q" else (k_f, k_parts)
                    nc.scalar.activation(full[:, :], misc[:, :], ACT.Identity, bias=bias)
                    wait(act, scr_out, (u + 1) * LOADS["scr"] * DMA)
                    nc.scalar.activation(parts[:, 0, :], misc[:, :], ACT.Identity, bias=bias).then_inc(misc_free, 1)
                elif name in ("q2", "k2"):
                    rest, parts = (q_r, q_parts) if name == "q2" else (k_r, k_parts)
                    act.wait_ge(rest_ready[name[0]], u + 2)
                    nc.scalar.activation(parts[:, 1, :], rest[:, :], ACT.Copy).then_inc(part_ready[name[0]], 1)
                elif name == "v":
                    act.wait_ge(misc_full, b.misc_use(name) + 1)
                    wait(act, vpad_ready, (u + 1) * NQ)
                    nc.scalar.activation(v_sb[:, :, :], misc_t, ACT.Copy).then_inc(misc_free, 1)
                elif name == "aT":
                    act.wait_ge(misc_full, b.misc_use(name) + 1)
                    if b.post == "B":
                        act.wait_ge(qb_in, (u - NA) * LOADS["qb"] * DMA)
                    bias = cols_a[:, 2:3] if b.post == "A" else w_post[:, W_POST - 3:W_POST - 2]
                    nc.scalar.activation(attn_T[:, :], misc[:, :], ACT.Identity, bias=bias).then_inc(misc_free, 1)
                elif name == "h2T":
                    v = u - 1
                    act.wait_ge(misc_full, b.misc_use(name) + 1)
                    wait(act, a_out, v * DMA * LOADS["a_out"])
                    cb, sb_col = mod_cols[:, 4, bass.ds(v, 1)], mod_cols[:, 3, bass.ds(v, 1)]
                    nc.scalar.activation(h2_T[:, :], misc[:, :], ACT.Identity, bias=sb_col, scale=cb, accum_out=h_sum[:, :])\
                      .then_inc(misc_free, 1)
                elif name == "gate":
                    act.wait_ge(lsh_ready, u)
                    nc.scalar.activation(lexp[:, :], lsh[:, :], ACT.Exp).then_inc(lexp_ready, 1)
                elif name == "x1T":
                    act.wait_ge(misc_full, b.misc_use(name) + 1)
                    nc.scalar.activation(x1_T[:, :], misc[:, :], ACT.Identity, bias=w_post[:, W_POST - 1:W_POST],
                                         scale=w_post[:, W_POST - 2:W_POST - 1]).then_inc(misc_free, 1)
                elif name in ("ff0", "ff1", "ff2", "ff3"):
                    c = int(name[2])
                    act.wait_ge(misc_full, b.misc_use(name) + 1)
                    nc.scalar.activation(hid[:, c, :], misc[:, :], ACT.Relu, 
                                         bias=w_post[:, W_POST - 3 - FC + c:W_POST - 3 - FC + c + 1]).then_inc(misc_free, 1)

            walk(act, half_step, item, pv_step)

        @block.tensor
        def _(pe):
            pe.wait_ge(silu_made, 1)
            for i in range(2):
                w = 3 * D
                nc.tensor.matmul(s_ps[0:NB, i, 0:w], c_s[:, :], w_mod[:, i * w:(i + 1) * w], start=True, stop=True)\
                  .then_inc(mod_mm, 1)
            for m in range(6):
                ins = nc.tensor.matmul(misc[:, m * NB:(m + 1) * NB], w_mod[:, m * D:(m + 1) * D], c_s[:, :],
                                       start=True, stop=True)
            ins.then_inc(mod_mm, 1)
            pe.wait_ge(consts_made, 1)
            pe.wait_ge(ones_made, 1)
            pe.wait_ge(consts_in, LOADS["const"] * DMA)
            pe.wait_ge(mod_made, 1)

            def score_tile(b, tick, c):
                knd, v = (b.steps, b.u) if tick < 8 else (b.prep, b.u + 1)
                if not knd:
                    return
                g = 2 + tick // T if tick < 8 else (tick - 8) // T
                t = tick % T
                n = b.u * NJ * TICKS + NJ * 8 + NJ * tick + c
                if t == 0 and c == 0:
                    pe.wait_ge(stk_in[g], (v + 1) * 2 * DMA)
                wait(pe, max_done, n - 1)
                bank = s_ps[:, c % 2, :]
                h = NJ * g + c
                keys = (t + 1) * P if knd == "A" else S
                ins = nc.tensor.matmul(bank[:, 0:keys], qstk[0:KROWS, h, t * P:(t + 1) * P], kstk[0:KROWS, h, 0:keys],
                                       start=True, stop=(knd == "B"))
                if knd == "A":
                    ins = nc.tensor.matmul(bank[:, t * P:keys], id_b[:, :], mask_q[:, :], start=False, stop=True)
                ins.then_inc(s_full, 1)

            def half_step(b, tick, half):
                for j in (2 * half, 2 * half + 1):
                    if b.steps:
                        n = b.u * 2 * TICKS + 2 * tick + half
                        g, key = tick // T, tick % T
                        if key == 0 and j == 0:
                            pe.wait_ge(off_in[g], (b.u + 1) * DMA)
                        if j % 2 == 0:
                            wait(pe, exp_done, n - 1)
                        lo = key * P if b.steps == "A" else 0
                        h = NJ * g + j
                        ins = nc.tensor.matmul(st_ps[:, j, lo:S], kstk[0:KALL, h, key * P:(key + 1) * P],
                                               qstk[0:KALL, h, lo:S], start=True, stop=(b.steps == "B"))
                        if b.steps == "A":
                            ins = nc.tensor.matmul(st_ps[:, j, lo:lo + P], id_b[:, :], mask_k[:, :], start=False, stop=True)
                        if j % 2 == 1:
                            ins.then_inc(st_full, 1)
                    score_tile(b, tick, j)

            def pv_step(b, tick):
                if (tick == 0 and not b.post) or (tick > 0 and not b.steps):
                    return
                unit, s, knd = (b.u - 1, TICKS - 1, b.post) if tick == 0 else (b.u, tick - 1, b.steps)
                g, key = s // T, s % T
                pe.wait_ge(exp_done, unit * 2 * TICKS + 2 * s + 2)
                if key == 0:
                    pe.wait_ge(vpad_ready, unit * NQ + g + 1)
                    if g % 2 == 0:
                        wait(pe, ev_done, unit * 2 + g // 2)
                lo = key * P if knd == "A" else 0
                for j in range(NJ):
                    ins = nc.tensor.matmul(pv_ps[32 * j:32 * j + 32, lo:S], vpad[:, key, g, j, :],
                                           probs[:, s % PBUF, j, lo:S], start=(key == 0 and g % 2 == 0),
                                           stop=(key == T - 1 and g % 2 == 1), tile_position=(0, 32 * j))
                ins.then_inc(pv_done, 1)

            def turn_off(b, v, g, name):
                pe.wait_ge(parts_ready, v * NQ + g + 1)
                wait(pe, misc_free, b.misc_use(name))
                for t in range(T):
                    ins = nc.tensor.transpose(misc_b[0:PARTS * NJ, t * P:(t + 1) * P],
                                              max_parts[:, g % 2, t, :, :].rearrange("p i j -> p (i j)"), id_b[:, :])
                ins.then_inc(misc_full, 1)

            def turn(b, name, src):
                wait(pe, misc_free, b.misc_use(name))
                for t in range(T):
                    ins = nc.tensor.transpose(misc[:, t * P:(t + 1) * P], src[:, t, :], id_f[:, :])
                ins.then_inc(misc_full, 1)

            def item(b, name):
                u = b.u
                w_qkv = w_a if b.prep == "A" else w_in
                if name == "off0":
                    turn_off(b, u + 1, 0, name)
                elif name in ("off1", "off2", "off3"):
                    turn_off(b, u, int(name[3]), name)
                elif name == "hT":
                    pe.wait_ge(norm_ready[0], u + 2)
                    turn(b, name, x_n)
                elif name in ("q", "k"):
                    if b.prep == "B" and name == "q":
                        pe.wait_ge(pb_in, (u + 2 - NA) * LOADS["pb"] * DMA)
                    wait(pe, misc_free, b.misc_use(name))
                    i = 0 if name == "q" else D
                    nc.tensor.matmul(misc[:, :], w_qkv[:, i:i + D], h_T[:, :], start=True, stop=True).then_inc(misc_full, 1)
                elif name == "v":
                    wait(pe, misc_free, b.misc_use(name))
                    for t in range(T):
                        ins = nc.tensor.matmul(misc[:, t * P:(t + 1) * P], h_T[:, t * P:(t + 1) * P], w_qkv[:, 2 * D:3 * D],
                                               start=True, stop=True)
                    ins.then_inc(misc_full, 1)
                elif name in ("O0", "O1"):
                    pe.wait_ge(ev_done, 2 * u)
                    wait(pe, misc_free, b.misc_use(name))
                    for i in range(2):
                        t = 2 * int(name[1]) + i
                        for gp in range(2):
                            ins = nc.tensor.transpose(misc[:, (2 * i + gp) * P:(2 * i + gp + 1) * P],
                                                      att_u[:, gp, t * P:(t + 1) * P], id_f[:, :])
                    ins.then_inc(misc_full, 1)
                elif name == "aT":
                    turn(b, name, attn)
                elif name in ("opA", "opB"):
                    w_o = w_a[:, 3 * D:4 * D] if name == "opA" else w_post[:, 0:D]
                    if name == "opB":
                        pe.wait_ge(qb_in, (u - NA) * LOADS["qb"] * DMA)
                    wait(pe, misc_free, b.misc_use(name))
                    for t in range(T):
                        ins = nc.tensor.matmul(misc[:, t * P:(t + 1) * P], attn_T[:, t * P:(t + 1) * P], w_o,
                                               start=True, stop=True)
                    ins.then_inc(misc_full, 1)
                elif name == "h2T":
                    pe.wait_ge(norm_ready[1], u)
                    turn(b, name, h2_n)
                elif name == "gate":
                    pe.wait_ge(hsum_ready, u)
                    wait(pe, misc_free, b.misc_use(name))
                    nc.tensor.matmul(misc[:, 0:NE], h_sum_b[:, :], gw[:, :], start=True, stop=True).then_inc(misc_full, 1)
                elif name == "x1T":
                    pe.wait_ge(norm_ready[2], u - NA)
                    turn(b, name, x1_n)
                elif name in ("ff0", "ff1", "ff2", "ff3"):
                    i = D + int(name[2]) * P
                    wait(pe, misc_free, b.misc_use(name))
                    nc.tensor.matmul(misc[:, :], w_post[:, i:i + P], x1_T[:, :], start=True, stop=True).then_inc(misc_full, 1)
                elif name == "out":
                    wait(pe, misc_free, b.misc_use(name))
                    for t in range(T):
                        for c in range(FC):
                            i = D + FF + c * D
                            ins = nc.tensor.matmul(misc[:, t * P:(t + 1) * P], hid[:, c, t * P:(t + 1) * P],
                                                   w_post[:, i:i + D], start=(c == 0), stop=(c == FC - 1))
                    ins.then_inc(misc_full, 1)

            walk(pe, half_step, item, pv_step)

        @block.vector
        def _(dve):
            v = nc.vector

            chain = Chain(dve, setup_chain, 22, 0)
            chain.link(v.memset(kstk[64:96, :, :], 1.0))
            chain.link(v.memset(vpad[:, :, :, :, :], 0.0))
            for g in range(NQ):
                i = (g % 2) * VW + HD
                chain.link(v.memset(vpad[:, :, g, :, i:i + 1], 1.0))
            for e in range(NE):
                chain.link(v.memset(before[:, e, :], 0.0))
                if e:
                    chain.link(v.memset(before[:, e, 0:e], 1.0))
                ins = v.memset(e_no[:, e:e + 1], float(e))
            ins.then_inc(ones_made, 1)
            dve.wait_ge(silu_exp, 1)
            chain.link(v.tensor_scalar(c_e[:, :], c_e[:, :], 1.0, None, ALU.add))
            chain.link(v.reciprocal(c_s[:, :], c_e[:, :]))
            v.tensor_tensor(c_s[:, :], c_s[:, :], c_T[:, :], ALU.mult).then_inc(silu_made, 1)
            dve.wait_ge(mod_mm, 3)
            chain.link(v.tensor_copy(mod_cols[:, :, :].rearrange("p m b -> p (m b)"), misc[:, 0:6 * NB]))
            v.tensor_scalar(mod_cols[:, 1:5:3, :], mod_cols[:, 1:5:3, :], 1.0, None, ALU.add)
            for i in range(2):
                chain.link(v.tensor_copy(mod4[:, 3 * i:3 * i + 3, :].rearrange("b m d -> b (m d)"), s_ps[0:NB, i, 0:3 * D]))
            g_mod = mod4[:, 2:6:3, :]
            chain.link(v.tensor_scalar(mod_a[:, :, :], g_mod, -1.0, None, ALU.mult))
            chain.link(v.scalar_tensor_tensor(out=mod_a[:, :, :], in0=mod_a[:, :, :], scalar=0.25, in1=g_mod,
                                              op0=ALU.max, op1=ALU.max))
            chain.link(v.tensor_scalar(mod_s[:, :, :], g_mod, 0.0, 2.0, ALU.is_ge, ALU.mult))
            chain.link(v.tensor_scalar(mod_s[:, :, :], mod_s[:, :, :], -1.0, None, ALU.add))
            chain.end()
            v.tensor_tensor(g_mod, mod_s[:, :, :], mod_a[:, :, :], ALU.mult).then_inc(mod_made, 1)

            def ln_stats(chain, i, src):
                for t in range(T):
                    ins = v.bn_stats(stats[:, i, t, :], src[:, t, :])
                chain.link(ins, bare_next=True)
                for t in range(T):
                    ins = v.bn_aggr(mv[:, i, t, :], stats[:, i, t, :])
                chain.link(ins)
                v.tensor_scalar(var_e[:, i, :], mv[:, i, :, 1], EPS, None, ALU.add).then_inc(var_ready[i], 1)

            def ln_end(chain, i, unit):
                dve.wait_ge(pow_ready[i], unit + 1)
                a, c = newton[:, i, 0, :], newton[:, i, 1, :]
                chain.link(v.tensor_tensor(a, rstd0[:, i, :], rstd0[:, i, :], ALU.mult))
                chain.link(v.tensor_tensor(c, a, var_e[:, i, :], ALU.mult))
                chain.link(v.tensor_scalar(a, c, -0.5, 1.5, ALU.mult, ALU.add))
                chain.link(v.tensor_tensor(rstd[:, i, :], a, rstd0[:, i, :], ALU.mult))
                chain.end()
                v.scalar_tensor_tensor(out=shift[:, i, :], in0=mv[:, i, :, 0], scalar=-1.0, in1=rstd[:, i, :],
                                       op0=ALU.mult, op1=ALU.mult).then_inc(rstd_ready[i], 1)

            def half_step(b, tick, half):
                knd, unit = (b.steps, b.u) if tick < 8 else (b.prep, b.u + 1)
                if not knd:
                    return
                g = 2 + tick // T if tick < 8 else (tick - 8) // T
                t = tick % T
                keys = (t + 1) * P if knd == "A" else S
                for c in (2 * half, 2 * half + 1):
                    n = b.u * NJ * TICKS + NJ * 8 + NJ * tick + c
                    dve.wait_ge(s_full, n + 1)
                    v.tensor_reduce(row_max[:, g % 2, t, c:c + 1], s_ps[:, c % 2, 0:keys], AX.X, ALU.max)\
                     .then_inc(max_done, 1)
                if t == T - 1 and half == 1:
                    q = g % 2
                    dve.wait_ge(max_done, n + 1)
                    chain = Chain(dve, parts_chain, 3, unit * NQ + g)
                    chain.link(v.tensor_scalar(max_parts[:, q, :, 0, :], row_max[:, q, :, :], -1.0, None, ALU.mult))
                    chain.link(v.scalar_tensor_tensor(out=max_r[:, q, :, :], in0=row_max[:, q, :, :], scalar=-1.0,
                                                      in1=max_parts[:, q, :, 0, :], op0=ALU.mult, op1=ALU.subtract))
                    chain.link(v.tensor_copy(max_parts[:, q, :, 1, :], max_r[:, q, :, :]))
                    chain.end()
                    v.tensor_tensor(max_parts[:, q, :, 2, :], max_r[:, q, :, :], max_parts[:, q, :, 1, :], ALU.subtract)\
                     .then_inc(parts_ready, 1)

            def pv_step(b, tick):
                pass

            open_chains = {}

            def item(b, name):
                u = b.u
                if name == "ln1a":
                    n = u + 1
                    dve.wait_ge(pa_in, (n + 1) * LOADS["pa"] * DMA)
                    open_chains["ln1"] = Chain(dve, ln1_chain, 6, n)
                    ln_stats(open_chains["ln1"], 0, x_in)
                elif name == "ln1b":
                    ln_end(open_chains["ln1"], 0, u + 1)
                elif name in ("O0", "O1"):
                    i = int(name[1])
                    src = misc[:, :].rearrange("p (h c) -> p h c", c=VW)
                    dve.wait_ge(misc_full, b.misc_use(name) + 1)
                    v.reciprocal(recip[:, i, :], src[:, :, HD]).then_inc(rec_done, 1)
                    dve.wait_ge(rec_done, (u - 1) * 2 + i + 1)
                    v.tensor_tensor(attn[:, 2 * i:2 * i + 2, :].rearrange("p t (h d) -> p (t h) d", d=HD), src[:, :, 0:HD],
                                    recip[:, i, :].unsqueeze(2).to_broadcast([P, 2 * NQ * NJ, HD]), ALU.mult)\
                     .then_inc(misc_free, 1)
                elif name == "opA":
                    n = u - 1
                    dve.wait_ge(misc_full, b.misc_use(name) + 1)
                    dve.wait_ge(pre_ready["A"], n + 1)
                    wait(dve, a_out, n * LOADS["a_out"] * DMA)
                    v.tensor_tensor(t1[:, :, :], misc_t, over_tiles(mod_post[:, 0, :]), ALU.mult).then_inc(misc_free, 1)
                    dve.wait_ge(misc_free, b.misc_use(name) + 1)
                    v.tensor_tensor(x2[:, :, :], t1[:, :, :], x_pre[:, :, :], ALU.add).then_inc(x2_ready, 1)
                    wait(dve, x2_ready, n + 1, bare=True)
                    c = open_chains["ln2"] = Chain(dve, ln2_chain, 6, n)
                    ln_stats(c, 1, x2)
                elif name == "ln2":
                    ln_end(open_chains["ln2"], 1, u - 1)
                elif name == "gsum":
                    dve.wait_ge(misc_free, b.misc_use("h2T") + 1)
                    v.tensor_copy(h_sum_b[:, :], h_sum[:, :].to_broadcast([P, P])).then_inc(hsum_ready, 1)
                elif name == "gate":
                    n = u - 1
                    dve.wait_ge(misc_full, b.misc_use(name) + 1)
                    v.scalar_tensor_tensor(out=lg[:, :], in0=misc[:, 0:NE], scalar=1.0 / S, in1=gb_b[:, :],
                                           op0=ALU.mult, op1=ALU.add).then_inc(misc_free, 1)
                    dve.wait_ge(misc_free, b.misc_use(name) + 1)
                    c = Chain(dve, gate_chain, 11, n)
                    c.link(v.tensor_reduce(lmax[:, :], lg[:, :], AX.X, ALU.max))
                    v.tensor_scalar(lsh[:, :], lg[:, :], lmax[:, 0:1], None, ALU.subtract).then_inc(lsh_ready, 1)
                    other = lg[:, :].unsqueeze(1).to_broadcast([P, NE, NE])
                    own = lg[:, :].unsqueeze(2).to_broadcast([P, NE, NE])
                    v.tensor_tensor(gt[:, :, :], other, own, ALU.is_gt)
                    c.link(v.tensor_tensor(eq[:, :, :], other, own, ALU.is_equal))
                    c.link(v.tensor_tensor(eq[:, :, :], eq[:, :, :], before[:, :, :], ALU.mult))
                    c.link(v.tensor_tensor(gt[:, :, :], gt[:, :, :], eq[:, :, :], ALU.add))
                    c.link(v.tensor_reduce(rank[:, :], gt[:, :, :], AX.X, ALU.add))
                    for k in range(TOPK):
                        ins = v.tensor_scalar(pick[:, k, :], rank[:, :], float(k), None, ALU.is_equal)
                    c.link(ins)
                    c.link(v.tensor_tensor(pick_n[:, :, :], pick[:, :, :], e_no[:, :].unsqueeze(1).to_broadcast([P, TOPK, NE]), ALU.mult))
                    c.link(v.tensor_reduce(nsel_f[:, :], pick_n[:, :, :], AX.X, ALU.add))
                    v.tensor_copy(nsel[:, bass.ds(n * TOPK, TOPK)], nsel_f[:, :])
                    dve.wait_ge(lexp_ready, n + 1)
                    c.link(v.tensor_reduce(lsum[:, :], lexp[:, :], AX.X, ALU.add))
                    c.link(v.reciprocal(lrec[:, :], lsum[:, :]))
                    c.link(v.scalar_tensor_tensor(out=pick_w[:, :, :], in0=pick[:, :, :], scalar=lrec[:, 0:1],
                                                  in1=lexp[:, :].unsqueeze(1).to_broadcast([P, TOPK, NE]),
                                                  op0=ALU.mult, op1=ALU.mult))
                    c.end()
                    v.tensor_reduce(wsel[:, bass.ds(n * TOPK, TOPK)], pick_w[:, :, :], AX.X, ALU.add).then_inc(sel_ready, 1)
                elif name in ("opB", "out"):
                    n = u - 1 - NA
                    dve.wait_ge(misc_full, b.misc_use(name) + 1)
                    if name == "opB":
                        i, ln, plus = 2, "ln3", x_pre
                        dve.wait_ge(pre_ready["B"], n + 1)
                    else:
                        i, ln, plus = 3, "ln4", x1
                        dve.wait_ge(x1_ready, n + 1)
                    v.tensor_tensor(t2[:, :, :], misc_t, plus[:, :, :], ALU.add).then_inc(misc_free, 1)
                    wait(dve, misc_free, b.misc_use(name) + 1, bare=True)
                    c = open_chains[ln] = Chain(dve, ln3_chain if ln == "ln3" else ln4_chain, 6, n)
                    ln_stats(c, i, t2)
                elif name in ("ln3", "ln4"):
                    ln_end(open_chains[name], 2 if name == "ln3" else 3, u - 1 - NA)

            walk(dve, half_step, item, pv_step)


def kernel(**inputs):
    import numpy as _np
    import concourse.bacc as _bacc
    from concourse import mybir as _mybir
    from concourse.bass_utils import run_bass_kernel_spmd as _run

    a = {k: _np.asarray(v) for k, v in inputs.items()}
    at = {k[len("L0_attn_"):]: v for k, v in a.items() if k.startswith("L0_attn_")}
    ff = {k[len("L0_ffn_"):]: v for k, v in a.items() if k.startswith("L0_ffn_")}
    ne = ff["gate_w"].shape[0]
    turned = lambda w: w.transpose(0, 2, 1)
    lin2 = turned(ff["lin2_w"]).reshape(ne, FC, P, D).transpose(0, 2, 1, 3).reshape(ne, P, FC * D)
    cat = _np.concatenate
    arrays = {
        "x": at["x"],
        "w_attn": cat([at["Wq"], at["Wk"], at["Wv"], at["Wmix"]], axis=1),
        "cols_attn": _np.stack([at["bq"], at["bk"], at["bv"]], axis=1),
        "row_attn": at["bmix"],
        "w_exp": cat([turned(ff["in_proj_w"]), turned(ff["in_proj_b"][:, 0:2 * D].reshape(ne, 2, D)),
                      turned(ff["out_proj_w"]), turned(ff["lin1_w"]), lin2,
                      turned(ff["lin1_b"].reshape(ne, FC, P)),
                      turned(_np.stack([ff["in_proj_b"][:, 2 * D:3 * D], ff["ln1_w"], ff["ln1_b"]], axis=1))], axis=2),
        "rows_exp": cat([ff["out_proj_b"], ff["ln1_w"], ff["ln1_b"], ff["lin2_b"],
                         ff["ln2_w"], ff["ln2_b"]], axis=1),
        "gate_wT": ff["gate_w"].T,
        "gate_b": ff["gate_b"],
        "cT": a["L0_c"].T,
        "wmod": a["L0_wmod"],
    }
    arrays = {f"in_{k}": _np.ascontiguousarray(v) for k, v in arrays.items()}
    nc = _bacc.Bacc("TRN2", target_bir_lowering=False, num_devices=1)
    args = [nc.dram_tensor(k, v.shape, _mybir.dt.from_np(v.dtype), kind="ExternalInput").ap() for k, v in arrays.items()]
    args.append(nc.dram_tensor("out_x", arrays["in_x"].shape, _mybir.dt.float32, kind="ExternalOutput").ap())
    adaln_kernel(nc, *args)
    r = _run(nc, [arrays], core_ids=[0])
    return r.results[0]["out_x"]
```

```python
from contextlib import ExitStack

import concourse.bass as bass
from concourse import mybir

F32 = mybir.dt.float32
BF16 = mybir.dt.bfloat16
I32 = mybir.dt.int32
ALU = mybir.AluOpType
ACT = mybir.ActivationFunctionType
AX = mybir.AxisListType

P = 128
NB, S, D = 4, 512, 128
HD = 8
T = S // P
NE, TOPK, FF = 4, 2, 512
FC = FF // P
NQ = 4
NJ = 4
PARTS = 3
KROWS = PARTS * PARTS * HD
KALL = KROWS + PARTS
VW = 16
TICKS = NQ * T
PBUF = 4
RING = 3
EPS = 1e-5
SCALE = HD ** -0.5
MASKED = -1e30
NA = NB
NU = NA + NB * TOPK
W_IN, W_POST = 3 * D + 2, D + FF + FC * D + FC + 3
DMA = 16


def kind(u):
    return "A" if u < NA else "B"


ATTN_ITEMS = [
    (0, 0, "mx1"), (0, 1, "off1"), (1, 0, "stk3"), (1, 0, "vp3"), (3, 3, "mx2"), (4, 1, "off2"),
    (7, 3, "mx3"), (9, 0, "off3"),
]
PREP_ITEMS = {
    "A": [
        (0, 1, "loadA"), (0, 2, "ln1a"), (1, 0, "ln1b"), (1, 0, "nm1"), (1, 2, "hT-"), (1, 2, "hT"),
        (3, 0, "q-"), (3, 0, "q"), (3, 2, "q2"), (3, 2, "scrq"), (4, 0, "k-"), (4, 0, "k"), (4, 2, "k2"),
        (5, 0, "v-"), (5, 0, "v"), (6, 0, "scrk"),
    ],
    "B": [
        (0, 1, "loadB"), (2, 0, "q-"), (2, 0, "q"), (2, 2, "q2"), (2, 2, "scrq"), (2, 3, "k-"),
        (2, 3, "k"), (3, 1, "k2"), (3, 1, "scrk"), (4, 0, "v-"), (4, 0, "v"),
    ],
    "all": [
        (6, 0, "stk0"), (8, 2, "vp0"), (9, 2, "stk1"), (10, 1, "vp1"), (12, 2, "mx0"), (12, 2, "stk2"),
        (14, 0, "off0"), (15, 3, "vp2"),
    ],
}
POST_ITEMS = {
    "A": [
        (0, 1, "loadPA"), (1, 1, "O0-"), (1, 1, "O0"), (3, 2, "O1-"), (3, 2, "O1"), (4, 1, "preA"),
        (5, 1, "aT-"), (5, 1, "aT"), (6, 3, "opA-"), (6, 3, "opA"), (6, 3, "st2"), (7, 1, "ln2"),
        (7, 1, "nm2"), (7, 3, "h2T-"), (7, 3, "h2T"), (8, 1, "gsum"), (8, 3, "gate"),
    ],
    "B": [
        (0, 2, "loadW"), (0, 2, "loadPB"), (1, 0, "O0-"), (1, 0, "O0"), (2, 1, "O1-"), (2, 1, "O1"),
        (2, 3, "preB"), (3, 2, "aT-"), (3, 2, "aT"), (4, 3, "opB-"), (4, 3, "opB"), (4, 3, "st3"),
        (5, 3, "ln3"), (7, 1, "nm3"), (8, 0, "x1T-"), (8, 0, "x1T"), (8, 1, "ff0-"), (8, 1, "ff0"),
        (8, 1, "ff1-"), (8, 1, "ff1"), (8, 3, "ff2-"), (8, 3, "ff2"), (9, 2, "ff3-"), (9, 2, "ff3"),
        (9, 3, "out---"), (10, 3, "out--"), (10, 3, "out-"), (10, 3, "out"), (11, 1, "st4"),
        (12, 1, "ln4"), (12, 3, "nm4"),
    ],
}
TENSOR_ORDER = (("T0",), ("T1", "S0", "S1", "T2", "P"), ("S2",), ("T3", "S3"))
PIECES = {"out": 4}
PV_SLOT = 1
MISC = ("off0", "off1", "off2", "off3", "hT", "q", "k", "v", "O0", "O1", "aT", "opA", "opB", "h2T",
        "gate", "x1T", "ff0", "ff1", "ff2", "ff3", "out")


class Body:

    def __init__(self, first, count, misc_base):
        self.first, self.count, self.misc_base = first, count, misc_base
        u = first
        self.steps = kind(u) if 0 <= u < NU else None
        self.prep = kind(u + 1) if u + 1 < NU else None
        self.post = kind(u - 1) if 0 <= u - 1 < NU else None
        items = []
        if self.prep:
            items += PREP_ITEMS[self.prep] + PREP_ITEMS["all"]
        if self.steps:
            items += ATTN_ITEMS
        if self.post:
            items += POST_ITEMS[self.post]
        self.items = sorted(items, key=lambda i: (i[0], i[1]))
        self.misc = [n for _, _, n in self.items if n in MISC]
        users = [n for _, _, n in self.items if n.rstrip("-") in MISC]
        assert all(users[i + 1] == n[:-1] for i, n in enumerate(users) if n[-1] == "-"), users

    def at(self, u):
        self.u = u
        self.misc_now = self.misc_base + (u - self.first) * len(self.misc)
        return self

    def misc_use(self, name):
        return self.misc_now + self.misc.index(name)


def bodies():
    out, base = [], 0
    for first, count in ((-1, 1), (0, 1), (1, 1), (2, 1), (3, 1), (4, 1), (5, 1), (6, NU - 7), (NU - 1, 1), (NU, 1)):
        out.append(Body(first, count, base))
        base += count * len(out[-1].misc)
    return out


def walk(eng, slot_step, item, pv_step):
    def emit(b):
        for tick in range(TICKS):
            for slot in range(NJ):
                slot_step(b, tick, slot)
                if slot == PV_SLOT:
                    pv_step(b, tick)
                for t, c, name in b.items:
                    if (t, c) == (tick, slot):
                        item(b, name)

    for b in bodies():
        if b.count == 1:
            emit(b.at(b.first))
        else:
            with eng.Fori(b.first, b.first + b.count) as u:
                emit(b.at(u))


def adaln_kernel(nc, x, w_attn, cols_attn, row_attn, w_exp, rows_exp, gate_wT, gate_b, cT, wmod, out):
    ctx = ExitStack()
    with ctx:
        def sb(name, shape, dt=F32):
            return ctx.enter_context(nc.sbuf_tensor(name, shape, dt))

        def pb(name, shape, dt=F32):
            return ctx.enter_context(nc.psum_tensor(name, shape, dt))

        def sem(name):
            return ctx.enter_context(nc.semaphore(name))

        kstk = sb("kstk", [P, NQ * NJ, S], BF16)
        qstk = sb("qstk", [P, NQ * NJ, S], BF16)
        probs = sb("probs", [P, PBUF, NJ, S])
        vpad = sb("vpad", [P, T, NQ, NJ, 2 * VW])
        v_sb = sb("v_sb", [P, T, D])
        att_u = sb("att_u", [P, 2, S])
        x_n = sb("x_n", [P, T, D])
        h_T = sb("h_T", [P, S])
        q_f = sb("q_f", [P, S])
        k_f = sb("k_f", [P, S])
        q_r = sb("q_r", [P, S])
        k_r = sb("k_r", [P, S])
        q_parts = sb("q_parts", [P, PARTS, S], BF16)
        k_parts = sb("k_parts", [P, PARTS, S], BF16)
        row_max = sb("row_max", [P, 2, T, NJ])
        max_r = sb("max_r", [P, 2, T, NJ])
        max_parts = sb("max_parts", [P, 2, T, PARTS, NJ], BF16)
        off_rows = sb("off_rows", [PARTS * NJ, 2, S], BF16)
        w_a = sb("w_a", [P, 4 * D])
        cols_a = sb("cols_a", [P, 3])
        row_a = sb("row_a", [P, D])
        w_in = sb("w_in", [P, W_IN])
        w_post = sb("w_post", [P, W_POST])
        rows_post = sb("rows_post", [P, 6, D])
        x_in = sb("x_in", [P, T, D])
        x_post = sb("x_post", [P, T, D])
        mod_post = sb("mod_post", [P, 3, D])
        gb_post = sb("gb_post", [P, D])
        h2_post = sb("h2_post", [P, T, D])
        recip = sb("recip", [P, 2, 2 * NQ * NJ])
        attn = sb("attn", [P, T, D])
        attn_T = sb("attn_T", [P, S])
        t1 = sb("t1", [P, T, D])
        x_pre = sb("x_pre", [P, T, D])
        row_t = sb("row_t", [P, D])
        row_w = sb("row_w", [P, D])
        row_g = sb("row_g", [P, D])
        h2_n = sb("h2_n", [P, T, D])
        x1_n = sb("x1_n", [P, T, D])
        y_n = sb("y_n", [P, T, D])
        out_pre = sb("out_pre", [P, T, D])
        t2 = sb("t2", [P, T, D])
        x2 = sb("x2", [P, T, D])
        h2 = sb("h2", [P, T, D])
        h2_T = sb("h2_T", [P, S])
        x1 = sb("x1", [P, T, D])
        x1_T = sb("x1_T", [P, S])
        hid = sb("hid", [P, FC, S])
        y = sb("y", [P, T, D])
        acc = sb("acc", [P, T, D])
        stats = sb("stats", [P, 4, T, 6])
        mv = sb("mv", [P, 4, T, 2])
        var_e = sb("var_e", [P, 4, T])
        rstd0 = sb("rstd0", [P, 4, T])
        newton = sb("newton", [P, 4, 2, T])
        minus_half = sb("minus_half", [P, T])
        rstd = sb("rstd", [P, 4, T])
        shift = sb("shift", [P, 4, T])
        h_sum = sb("h_sum", [P, 1])
        h_sum_b = sb("h_sum_b", [P, P])
        gw = sb("gw", [P, NE])
        gb_b = sb("gb_b", [P, NE])
        before = sb("before", [P, NE, NE])
        e_no = sb("e_no", [P, NE])
        lg = sb("lg", [P, NE])
        lmax = sb("lmax", [P, 1])
        lsh = sb("lsh", [P, NE])
        lexp = sb("lexp", [P, NE])
        lsum = sb("lsum", [P, 1])
        lrec = sb("lrec", [P, 1])
        gt = sb("gt", [P, NE, NE])
        eq = sb("eq", [P, NE, NE])
        rank = sb("rank", [P, NE])
        pick = sb("pick", [P, TOPK, NE])
        pick_w = sb("pick_w", [P, TOPK, NE])
        pick_n = sb("pick_n", [P, TOPK, NE])
        nsel_f = sb("nsel_f", [P, TOPK])
        wsel = sb("wsel", [P, NB * TOPK])
        nsel = sb("nsel", [P, NB * TOPK], I32)
        c_T = sb("c_T", [P, NB])
        c_e = sb("c_e", [P, NB])
        c_s = sb("c_s", [P, NB])
        w_mod = sb("w_mod", [P, 6 * D])
        mod4 = sb("mod4", [NB, 6, D])
        mod_a = sb("mod_a", [NB, 2, D])
        mod_s = sb("mod_s", [NB, 2, D])
        mod_cols = sb("mod_cols", [P, 6, NB])
        zeros = sb("zeros", [P, P])
        ones_row = sb("ones_row", [P, D])
        id_f = sb("id_f", [P, P])
        id_b = sb("id_b", [P, P], BF16)
        mask_q = sb("mask_q", [P, P], BF16)
        mask_k = sb("mask_k", [P, P], BF16)
        neg = sb("neg", [P, P], BF16)

        st_ps = pb("st_ps", [P, RING, S])
        s_ps = pb("s_ps", [P, RING, S])
        pv_ps = pb("pv_ps", [P, S])
        misc = pb("misc", [P, S])
        misc_b = misc[:, :].bitcast(BF16)
        misc_t = misc[:, :].rearrange("p (t d) -> p t d", t=T)

        stk_shape = [NQ * NJ, PARTS, PARTS, HD, S]
        q_dram = nc.dram_tensor("q_scratch", stk_shape, BF16).ap()
        k_dram = nc.dram_tensor("k_scratch", stk_shape, BF16).ap()
        mod_dram = nc.dram_tensor("mod_scratch", [NB, 6 * D], F32).ap()
        h2_dram = nc.dram_tensor("h2_scratch", [NB, S, D], F32).ap()
        h2T_dram = nc.dram_tensor("h2T_scratch", [NB, P, S], F32).ap()

        def hidden_bank(b, c):
            if b.steps:
                return misc[:, :]
            return st_ps[:, c, :] if c < RING else s_ps[:, c - RING, :]

        def tokens(a):
            return a.rearrange("(t p) d -> p t d", p=P)

        q_rows = q_dram.rearrange("(gp j sub) a i d n -> gp sub (a i d) j n", gp=2, j=NJ)
        k_rows = k_dram.rearrange("(gp j sub) a i d n -> gp sub (a i d) j n", gp=2, j=NJ)

        consts_in = sem("consts_in")
        cmod_in = sem("cmod_in")
        consts_made = sem("consts_made")
        ones_made = sem("ones_made")
        setup_chain = sem("setup_chain")
        setup_pool = sem("setup_pool")
        silu_exp = sem("silu_exp")
        silu_made = sem("silu_made")
        mod_mm = sem("mod_mm")
        cols_made = sem("cols_made")
        mod_made = sem("mod_made")
        mod_out = sem("mod_out")
        st_full = sem("st_full")
        exp_done = sem("exp_done")
        s_full = sem("s_full")
        max_done = sem("max_done")
        parts_ready = sem("parts_ready")
        parts_chain = sem("parts_chain")
        off_in = [sem(f"off{g}_in") for g in range(NQ)]
        pv_done = sem("pv_done")
        ev_done = sem("ev_done")
        misc_full = sem("misc_full")
        misc_free = sem("misc_free")
        ln1_chain = sem("ln1_chain")
        ln2_chain = sem("ln2_chain")
        ln3_chain = sem("ln3_chain")
        ln4_chain = sem("ln4_chain")
        var_ready = [sem(f"var{i}_ready") for i in range(4)]
        pow_ready = [sem(f"pow{i}_ready") for i in range(4)]
        rstd_ready = [sem(f"rstd{i}_ready") for i in range(4)]
        norm_ready = [sem(f"norm{i}_ready") for i in range(4)]
        rest_ready = {n: sem(f"{n}_rest_ready") for n in "qk"}
        part_ready = {n: sem(f"{n}_part_ready") for n in "qk"}
        split = {n: sem(f"{n}_split") for n in "qk"}
        scr_out = sem("scr_out")
        stk_in = [sem(f"stk{g}_in") for g in range(NQ)]
        vpad_ready = sem("vpad_ready")
        pa_in = sem("pa_in")
        pb_in = sem("pb_in")
        qa_in = sem("qa_in")
        wp_in = sem("wp_in")
        qb_in = sem("qb_in")
        rec_done = sem("rec_done")
        x2_ready = sem("x2_ready")
        h2_ready = sem("h2_ready")
        hsum_ready = sem("hsum_ready")
        pre_ready = {k: sem(f"pre{k}_ready") for k in "AB"}
        pre_chain = sem("pre_chain")
        h2_chain = sem("h2_chain")
        x1_chain = sem("x1_chain")
        y_chain = sem("y_chain")
        gate_chain = sem("gate_chain")
        lsh_ready = sem("lsh_ready")
        lexp_ready = sem("lexp_ready")
        sel_ready = sem("sel_ready")
        a_out = sem("a_out")
        x1_ready = sem("x1_ready")
        acc_ready = sem("acc_ready")
        b_out = sem("b_out")

        LOADS = {"pa": 1, "pb": 2, "qa": 2, "qb": 4, "a_out": 3, "const": 5, "scr": 2 * PARTS * PARTS}

        block = ctx.enter_context(nc.Block())

        def wait(eng, s, value, bare=False):
            if isinstance(value, int):
                if value > 0:
                    eng.wait_ge(s, value)
                return
            if bare or eng.engine == nc.sync.engine:
                value = eng.to_reg(value)
                true_since_setup, n = {nc.sync.engine: (mod_out, DMA), nc.gpsimd.engine: (consts_made, 1),
                                       nc.vector.engine: (silu_exp, 1)}[eng.engine]
                eng.wait_ge(true_since_setup, n)
            eng.wait_ge(s, value)

        def over_tiles(row):
            return row.unsqueeze(1).to_broadcast([P, T, D])

        class Chain:

            def __init__(self, eng, s, per, unit):
                self.eng, self.s, self.per, self.base, self.n = eng, s, per, unit * per, 0

            def link(self, ins, bare_next=False):
                self.n += 1
                ins.then_inc(self.s, 1)
                wait(self.eng, self.s, self.base + self.n, bare_next)

            def end(self):
                assert self.n == self.per, (self.n, self.per)

        @block.sync
        def _(sp):
            sp.dma_start(c_T[:, :], cT).then_inc(cmod_in, DMA)
            sp.dma_start(w_mod[:, :], wmod).then_inc(cmod_in, DMA)
            sp.dma_start(x_in[:, :, :], tokens(x[0])).then_inc(pa_in, DMA)
            sp.dma_start(w_a[:, :], w_attn).then_inc(consts_in, DMA)
            sp.dma_start(cols_a[:, :], cols_attn).then_inc(consts_in, DMA)
            sp.dma_start(row_a[:, :], row_attn.partition_broadcast(P)).then_inc(consts_in, DMA)
            sp.dma_start(gw[:, :], gate_wT).then_inc(consts_in, DMA)
            sp.dma_start(gb_b[:, :], gate_b.partition_broadcast(P)).then_inc(consts_in, DMA)
            def store_modulation():
                sp.wait_ge(mod_made, 1)
                sp.dma_start(mod_dram, mod4[:, :, :].rearrange("b m d -> b (m d)")).then_inc(mod_out, DMA)

            def slot_step(b, tick, slot):
                pass

            def pv_step(b, tick):
                pass

            def load_stack(v, g):
                wait(sp, st_full, (v - 1) * NJ * TICKS + NJ * T * (g + 1))
                wait(sp, s_full, (v - 1) * NJ * TICKS + NJ * T * (g + 1))
                for dst, src in ((qstk, q_rows), (kstk, k_rows)):
                    sp.dma_start(dst[0:KROWS, NJ * g:NJ * g + NJ, :], src[g // 2, g % 2]).then_inc(stk_in[g], DMA)

            def load_off(b, v, g, name):
                wait(sp, misc_free, b.misc_use(name) + 1)
                sp.dma_start(qstk[KROWS:KALL, NJ * g:NJ * g + NJ, :], off_rows[:, g % 2, :]).then_inc(off_in[g], DMA)

            def part_made(b, name, i):
                if i == 0:
                    wait(sp, misc_free, b.misc_use(name) + 1)
                else:
                    wait(sp, (part_ready if i == 1 else split)[name], b.u + 2)

            def item(b, name):
                u = b.u
                if name == "stk3":
                    load_stack(u, 3)
                elif name in ("stk0", "stk1", "stk2"):
                    if b.first < 0 and name == "stk0":
                        sp.wait_ge(ones_made, 1)
                        sp.wait_ge(mod_out, DMA)
                    load_stack(u + 1, int(name[3]))
                elif name == "off0":
                    load_off(b, u + 1, 0, name)
                elif name in ("off1", "off2", "off3"):
                    load_off(b, u, int(name[3]), name)
                elif name == "loadA" and b.first >= 0:
                    v = u + 1
                    wait(sp, norm_ready[0], v)
                    sp.dma_start(x_in[:, :, :], tokens(x[v])).then_inc(pa_in, DMA)
                elif name == "loadB":
                    w = u + 1 - NA
                    wait(sp, sel_ready, w // TOPK + 1)
                    wait(sp, a_out, (w // TOPK + 1) * LOADS["a_out"] * DMA)
                    e = sp.value_load(nsel[0:1, bass.ds(w, 1)], min_val=0, max_val=NE - 1)
                    wait(sp, vpad_ready, (w + NA) * NQ - 1)
                    sp.dma_start(h_T[:, :], h2T_dram[w // TOPK]).then_inc(pb_in, DMA)
                    sp.dma_start(w_in[:, :], w_exp[e, :, 0:W_IN]).then_inc(pb_in, DMA)
                elif name == "scrq":
                    v = u + 1
                    for g in range(NQ):
                        wait(sp, stk_in[g], v * 2 * DMA)
                    for i in range(PARTS):
                        part_made(b, "q", i)
                        for a in range(PARTS):
                            sp.dma_start(q_dram[:, a, i], q_parts[:, i, :]).then_inc(scr_out, DMA)
                    if b.first < 0:
                        store_modulation()
                elif name == "scrk":
                    v = u + 1
                    for a in range(PARTS):
                        part_made(b, "k", a)
                        for i in range(PARTS):
                            sp.dma_start(k_dram[:, a, i], k_parts[:, a, :]).then_inc(scr_out, DMA)
                    wait(sp, scr_out, (v + 1) * LOADS["scr"] * DMA)
                elif name == "loadPA":
                    v = u - 1
                    wait(sp, h2_ready, v)
                    sp.dma_start(x_post[:, :, :], tokens(x[v])).then_inc(qa_in, DMA)
                    sp.dma_start(mod_post[:, :, :].rearrange("p m d -> p (m d)"),
                                 mod_dram[v, 2 * D:5 * D].partition_broadcast(P)).then_inc(qa_in, DMA)
                elif name == "loadW":
                    w = u - 1 - NA
                    wait(sp, var_ready[3], w)
                    e = sp.value_load(nsel[0:1, bass.ds(w, 1)], min_val=0, max_val=NE - 1)
                    sp.dma_start(w_post[:, :], w_exp[e, :, W_IN:W_IN + W_POST]).then_inc(wp_in, DMA)
                elif name == "loadPB":
                    w = u - 1 - NA
                    if isinstance(w, int) and w == 0:
                        wait(sp, a_out, NA * LOADS["a_out"] * DMA)
                    else:
                        wait(sp, b_out, w * DMA)
                    e = sp.value_load(nsel[0:1, bass.ds(w, 1)], min_val=0, max_val=NE - 1)
                    sp.dma_start(rows_post[:, :, :].rearrange("p m d -> p (m d)"),
                                 rows_exp[e].partition_broadcast(P)).then_inc(qb_in, DMA)
                    sp.dma_start(gb_post[:, :], mod_dram[w // TOPK, 5 * D:6 * D].partition_broadcast(P))\
                      .then_inc(qb_in, DMA)
                    sp.dma_start(h2_post[:, :, :], tokens(h2_dram[w // TOPK])).then_inc(qb_in, DMA)
                    sp.dma_start(x_post[:, :, :], tokens(out[w // TOPK])).then_inc(qb_in, DMA)
                elif name == "h2T":
                    v = u - 1
                    wait(sp, x2_ready, v + 1)
                    sp.dma_start(tokens(out[v]), x2[:, :, :]).then_inc(a_out, DMA)
                    wait(sp, misc_free, b.misc_use(name) + 1)
                    sp.dma_start(h2T_dram[v], h2_T[:, :]).then_inc(a_out, DMA)
                    wait(sp, h2_ready, v + 1)
                    sp.dma_start(tokens(h2_dram[v]), h2[:, :, :]).then_inc(a_out, DMA)
                elif name == "nm4":
                    w = u - 1 - NA
                    wait(sp, acc_ready, w + 1)
                    sp.dma_start(tokens(out[w // TOPK]), acc[:, :, :]).then_inc(b_out, DMA)

            walk(sp, slot_step, item, pv_step)
            sp.wait_ge(b_out, NB * TOPK * DMA)

        @block.gpsimd
        def _(pool):
            chain = Chain(pool, setup_pool, 7, 0)
            nc.gpsimd.memset(ones_row[:, :], 1.0)
            chain.link(nc.gpsimd.memset(id_f[:, :], 0.0))
            chain.link(nc.gpsimd.memset(zeros[:, :], 0.0))
            chain.link(nc.gpsimd.affine_select(out=id_f[:, :], in_=id_f[:, :], compare_op=ALU.not_equal, fill=1.0,
                                               base=0, pattern=[[-1, P]], channel_multiplier=1))
            chain.link(nc.gpsimd.tensor_copy(id_b[:, :], id_f[:, :]))
            chain.link(nc.gpsimd.affine_select(out=neg[:, :], in_=zeros[:, :], compare_op=ALU.is_ge, fill=MASKED,
                                               base=0, pattern=[[-1, P]], channel_multiplier=1))
            chain.link(nc.gpsimd.tensor_copy(mask_q[:, :], neg[:, :]))
            chain.link(nc.gpsimd.affine_select(out=mask_k[:, :], in_=zeros[:, :], compare_op=ALU.is_ge, fill=MASKED,
                                               base=0, pattern=[[1, P]], channel_multiplier=-1))
            chain.end()
            nc.gpsimd.memset(minus_half[:, :], -0.5).then_inc(consts_made, 1)
            pool.wait_ge(consts_made, 1)

            def slot_step(b, tick, slot):
                pass

            def pv_step(b, tick):
                pass

            pool_tt = nc.gpsimd.tensor_tensor

            def power(i, unit):
                pool.wait_ge(var_ready[i], unit + 1)
                nc.gpsimd.tensor_tensor(rstd0[:, i, :], var_e[:, i, :], minus_half[:, :], ALU.pow)\
                  .then_inc(pow_ready[i], 1)

            def place_v(v, g):
                gp, sub = g // 2, g % 2
                wait(pool, pv_done, (v - 1) * TICKS + T * (g + 1), bare=True)
                nc.gpsimd.tensor_copy(
                    vpad[:, :, g, :, sub * VW:sub * VW + HD],
                    v_sb[:, :, :].rearrange("p k (gp j sub d) -> p k gp j sub d", gp=2, j=NJ, sub=2)[:, :, gp, :, sub, :],
                ).then_inc(vpad_ready, 1)

            def item(b, name):
                u = b.u
                if name == "ln1a":
                    power(0, u + 1)
                elif name == "st2":
                    power(1, u - 1)
                elif name == "st3":
                    power(2, u - 1 - NA)
                elif name == "st4":
                    power(3, u - 1 - NA)
                elif name in ("q", "k"):
                    full, rest, parts = (q_f, q_r, q_parts) if name == "q" else (k_f, k_r, k_parts)
                    wait(pool, misc_free, b.misc_use(name) + 1)
                    pool_tt(rest[:, :], full[:, :], parts[:, 0, :], ALU.subtract).then_inc(rest_ready[name], 1)
                elif name in ("q2", "k2"):
                    rest, parts = (q_r, q_parts) if name == "q2" else (k_r, k_parts)
                    wait(pool, part_ready[name[0]], u + 2)
                    pool_tt(parts[:, 2, :], rest[:, :], parts[:, 1, :], ALU.subtract).then_inc(split[name[0]], 1)
                elif name == "preA":
                    pool.wait_ge(qa_in, u * LOADS["qa"] * DMA)
                    c = Chain(pool, pre_chain, 1, u - 1)
                    c.link(pool_tt(row_t[:, :], row_a[:, :], mod_post[:, 0, :], ALU.mult))
                    pool_tt(x_pre[:, :, :], x_post[:, :, :], over_tiles(row_t[:, :]), ALU.add).then_inc(pre_ready["A"], 1)
                elif name == "nm2":
                    n = u - 1
                    wait(pool, a_out, n * LOADS["a_out"] * DMA)
                    c = Chain(pool, h2_chain, 2, n)
                    c.link(pool_tt(row_w[:, :], mod_post[:, 2, :], ones_row[:, :], ALU.add))
                    wait(pool, norm_ready[1], n + 1)
                    c.link(pool_tt(h2[:, :, :], h2_n[:, :, :], over_tiles(row_w[:, :]), ALU.mult))
                    c.end()
                    pool_tt(h2[:, :, :], h2[:, :, :], over_tiles(mod_post[:, 1, :]), ALU.add).then_inc(h2_ready, 1)
                elif name == "preB":
                    pool.wait_ge(qb_in, (u - NA) * LOADS["qb"] * DMA)
                    pool_tt(x_pre[:, :, :], h2_post[:, :, :], over_tiles(rows_post[:, 0, :]), ALU.add)\
                        .then_inc(pre_ready["B"], 1)
                elif name == "nm3":
                    n = u - 1 - NA
                    pool_tt(row_t[:, :], rows_post[:, 2, :], rows_post[:, 3, :], ALU.add)
                    wait(pool, norm_ready[2], n + 1)
                    c = Chain(pool, x1_chain, 1, n)
                    c.link(pool_tt(x1[:, :, :], x1_n[:, :, :], over_tiles(rows_post[:, 1, :]), ALU.mult))
                    c.end()
                    pool_tt(x1[:, :, :], x1[:, :, :], over_tiles(row_t[:, :]), ALU.add).then_inc(x1_ready, 1)
                elif name == "nm4":
                    n = u - 1 - NA
                    c = Chain(pool, y_chain, 4, n)
                    c.link(pool_tt(row_g[:, :], gb_post[:, :], wsel[:, bass.ds(n, 1)].to_broadcast([P, D]), ALU.mult))
                    pool_tt(row_w[:, :], rows_post[:, 4, :], row_g[:, :], ALU.mult)
                    c.link(pool_tt(row_t[:, :], rows_post[:, 5, :], row_g[:, :], ALU.mult))
                    c.link(pool_tt(out_pre[:, :, :], x_post[:, :, :], over_tiles(row_t[:, :]), ALU.add))
                    wait(pool, norm_ready[3], n + 1)
                    c.link(pool_tt(y[:, :, :], y_n[:, :, :], over_tiles(row_w[:, :]), ALU.mult))
                    c.end()
                    pool_tt(acc[:, :, :], y[:, :, :], out_pre[:, :, :], ALU.add).then_inc(acc_ready, 1)
                elif name == "vp3":
                    place_v(u, 3)
                elif name in ("vp0", "vp1", "vp2"):
                    if name == "vp0":
                        wait(pool, misc_free, b.misc_use("v") + 1, bare=True)
                        wait(pool, ones_made, 1)
                    place_v(u + 1, int(name[2]))

            walk(pool, slot_step, item, pv_step)

        @block.scalar
        def _(act):
            act.wait_ge(cmod_in, 2 * DMA)
            nc.scalar.activation(c_e[:, :], c_T[:, :], ACT.Exp, scale=-1.0).then_inc(silu_exp, 1)

            def slot_step(b, tick, slot):
                if not b.steps:
                    return
                n = b.u * NJ * TICKS + NJ * tick + slot
                key = tick % T
                lo = key * P if b.steps == "A" else 0
                act.wait_ge(st_full, n + 1)
                if slot == 0:
                    wait(act, pv_done, b.u * TICKS + tick - (PBUF - 1))
                nc.scalar.activation(probs[:, tick % PBUF, slot, lo:S], st_ps[:, (NJ * tick + slot) % RING, lo:S],
                                     ACT.Exp, scale=SCALE).then_inc(exp_done, 1)

            def pv_step(b, tick):
                gp = {8: 0, 0: 1}.get(tick)
                if gp is None or (gp == 0 and not b.steps) or (gp == 1 and not b.post):
                    return
                unit = b.u if gp == 0 else b.u - 1
                act.wait_ge(pv_done, unit * TICKS + 8 * (gp + 1))
                nc.scalar.activation(att_u[:, gp, :], pv_ps[:, :], ACT.Copy).then_inc(ev_done, 1)

            def normalise(i, unit, dst, src):
                act.wait_ge(rstd_ready[i], unit + 1)
                for t in range(T):
                    ins = nc.scalar.activation(dst[:, t, :], src[:, t, :], ACT.Identity, bias=shift[:, i, t:t + 1],
                                               scale=rstd[:, i, t:t + 1])
                ins.then_inc(norm_ready[i], 1)

            def copy_off(b, v, g, name):
                act.wait_ge(misc_full, b.misc_use(name) + 1)
                wait(act, off_in[(g - 2) % NQ], (v + (g >= 2)) * DMA)
                nc.scalar.activation(off_rows[:, g % 2, :], misc_b[0:PARTS * NJ, 0:S], ACT.Copy).then_inc(misc_free, 1)

            def item(b, name):
                u = b.u
                if name == "off0":
                    copy_off(b, u + 1, 0, name)
                elif name in ("off1", "off2", "off3"):
                    copy_off(b, u, int(name[3]), name)
                elif name == "nm1":
                    normalise(0, u + 1, x_n, x_in)
                elif name == "nm2":
                    wait(act, h2_ready, u - 1)
                    normalise(1, u - 1, h2_n, x2)
                elif name == "nm3":
                    wait(act, x1_ready, u - 1 - NA)
                    normalise(2, u - 1 - NA, x1_n, t2)
                elif name == "nm4":
                    wait(act, acc_ready, u - 1 - NA)
                    normalise(3, u - 1 - NA, y_n, t2)
                elif name == "hT":
                    act.wait_ge(misc_full, b.misc_use(name) + 1)
                    ca, sa = mod_cols[:, 1, bass.ds(u + 1, 1)], mod_cols[:, 0, bass.ds(u + 1, 1)]
                    nc.scalar.activation(h_T[:, :], misc[:, :], ACT.Identity, bias=sa, scale=ca).then_inc(misc_free, 1)
                elif name in ("q", "k"):
                    act.wait_ge(misc_full, b.misc_use(name) + 1)
                    col = 0 if name == "q" else 1
                    bias = cols_a[:, col:col + 1] if b.prep == "A" else w_in[:, 3 * D + col:3 * D + col + 1]
                    full, parts = (q_f, q_parts) if name == "q" else (k_f, k_parts)
                    nc.scalar.activation(full[:, :], misc[:, :], ACT.Identity, bias=bias)
                    wait(act, scr_out, (u + 1) * LOADS["scr"] * DMA)
                    nc.scalar.activation(parts[:, 0, :], misc[:, :], ACT.Identity, bias=bias).then_inc(misc_free, 1)
                elif name in ("q2", "k2"):
                    rest, parts = (q_r, q_parts) if name == "q2" else (k_r, k_parts)
                    act.wait_ge(rest_ready[name[0]], u + 2)
                    nc.scalar.activation(parts[:, 1, :], rest[:, :], ACT.Copy).then_inc(part_ready[name[0]], 1)
                elif name == "v":
                    act.wait_ge(misc_full, b.misc_use(name) + 1)
                    wait(act, vpad_ready, (u + 1) * NQ)
                    nc.scalar.activation(v_sb[:, :, :], misc_t, ACT.Copy).then_inc(misc_free, 1)
                elif name == "aT":
                    act.wait_ge(misc_full, b.misc_use(name) + 1)
                    if b.post == "B":
                        act.wait_ge(wp_in, (u - NA) * DMA)
                    bias = cols_a[:, 2:3] if b.post == "A" else w_post[:, W_POST - 3:W_POST - 2]
                    nc.scalar.activation(attn_T[:, :], misc[:, :], ACT.Identity, bias=bias).then_inc(misc_free, 1)
                elif name == "h2T":
                    v = u - 1
                    act.wait_ge(misc_full, b.misc_use(name) + 1)
                    wait(act, a_out, v * DMA * LOADS["a_out"])
                    cb, sb_col = mod_cols[:, 4, bass.ds(v, 1)], mod_cols[:, 3, bass.ds(v, 1)]
                    nc.scalar.activation(h2_T[:, :], misc[:, :], ACT.Identity, bias=sb_col, scale=cb, accum_out=h_sum[:, :])\
                      .then_inc(misc_free, 1)
                elif name == "gate":
                    act.wait_ge(lsh_ready, u)
                    nc.scalar.activation(lexp[:, :], lsh[:, :], ACT.Exp).then_inc(lexp_ready, 1)
                elif name == "x1T":
                    act.wait_ge(misc_full, b.misc_use(name) + 1)
                    nc.scalar.activation(x1_T[:, :], misc[:, :], ACT.Identity, bias=w_post[:, W_POST - 1:W_POST],
                                         scale=w_post[:, W_POST - 2:W_POST - 1]).then_inc(misc_free, 1)
                elif name in ("ff0", "ff1", "ff2", "ff3"):
                    c = int(name[2])
                    act.wait_ge(misc_full, b.misc_use(name) + 1)
                    nc.scalar.activation(hid[:, c, :], hidden_bank(b, c), ACT.Relu, 
                                         bias=w_post[:, W_POST - 3 - FC + c:W_POST - 3 - FC + c + 1]).then_inc(misc_free, 1)

            walk(act, slot_step, item, pv_step)

        @block.tensor
        def _(pe):
            pe.wait_ge(silu_made, 1)
            for m in range(6):
                ins = nc.tensor.matmul(misc[:, m * NB:(m + 1) * NB], w_mod[:, m * D:(m + 1) * D], c_s[:, :],
                                       start=True, stop=True)
            ins.then_inc(mod_mm, 1)
            for i in range(2):
                w = 3 * D
                nc.tensor.matmul(s_ps[0:NB, i, 0:w], c_s[:, :], w_mod[:, i * w:(i + 1) * w], start=True, stop=True)\
                  .then_inc(mod_mm, 1)
            pe.wait_ge(consts_made, 1)
            pe.wait_ge(consts_in, LOADS["const"] * DMA)
            pe.wait_ge(cols_made, 1)

            def score_tile(b, tick, c):
                knd, v = (b.steps, b.u) if tick < 8 else (b.prep, b.u + 1)
                if not knd:
                    return
                g = 2 + tick // T if tick < 8 else (tick - 8) // T
                t = tick % T
                n = b.u * NJ * TICKS + NJ * 8 + NJ * tick + c
                if t == 0 and c == 0:
                    if b.first < 0 and g == 0:
                        pe.wait_ge(mod_made, 1)
                        pe.wait_ge(ones_made, 1)
                    pe.wait_ge(stk_in[g], (v + 1) * 2 * DMA)
                i = NJ * tick + c
                wait(pe, max_done, n - (RING - 1 if i else 0))
                bank = s_ps[:, i % RING, :]
                h = NJ * g + c
                keys = (t + 1) * P if knd == "A" else S
                ins = nc.tensor.matmul(bank[:, 0:keys], qstk[0:KROWS, h, t * P:(t + 1) * P], kstk[0:KROWS, h, 0:keys],
                                       start=True, stop=(knd == "B"))
                if knd == "A":
                    ins = nc.tensor.matmul(bank[:, t * P:keys], id_b[:, :], mask_q[:, :], start=False, stop=True)
                ins.then_inc(s_full, 1)

            def key_scores(b, tick, j):
                if b.steps:
                    g, key = tick // T, tick % T
                    if key == 0 and j == 0:
                        pe.wait_ge(off_in[g], (b.u + 1) * DMA)
                    i = NJ * tick + j
                    wait(pe, exp_done, b.u * NJ * TICKS + i - (RING - 1 if i else 0))
                    lo = key * P if b.steps == "A" else 0
                    h = NJ * g + j
                    ins = nc.tensor.matmul(st_ps[:, i % RING, lo:S], kstk[0:KALL, h, key * P:(key + 1) * P],
                                           qstk[0:KALL, h, lo:S], start=True, stop=(b.steps == "B"))
                    if b.steps == "A":
                        ins = nc.tensor.matmul(st_ps[:, i % RING, lo:lo + P], id_b[:, :], mask_k[:, :], start=False, stop=True)
                    ins.then_inc(st_full, 1)

            def slot_step(b, tick, slot):
                for op in TENSOR_ORDER[slot]:
                    if op == "P":
                        attention_product(b, tick)
                    else:
                        {"T": key_scores, "S": score_tile}[op[0]](b, tick, int(op[1]))

            def pv_step(b, tick):
                pass

            def attention_product(b, tick):
                if (tick == 0 and not b.post) or (tick > 0 and not b.steps):
                    return
                unit, s, knd = (b.u - 1, TICKS - 1, b.post) if tick == 0 else (b.u, tick - 1, b.steps)
                g, key = s // T, s % T
                pe.wait_ge(exp_done, unit * NJ * TICKS + NJ * (s + 1))
                if key == 0:
                    pe.wait_ge(vpad_ready, unit * NQ + g + 1)
                    if g % 2 == 0:
                        wait(pe, ev_done, unit * 2 + g // 2)
                lo = key * P if knd == "A" else 0
                for j in range(NJ):
                    ins = nc.tensor.matmul(pv_ps[32 * j:32 * j + 32, lo:S], vpad[:, key, g, j, :],
                                           probs[:, s % PBUF, j, lo:S], start=(key == 0 and g % 2 == 0),
                                           stop=(key == T - 1 and g % 2 == 1), tile_position=(0, 32 * j))
                ins.then_inc(pv_done, 1)

            def turn_off(b, v, g, name):
                pe.wait_ge(parts_ready, v * NQ + g + 1)
                wait(pe, misc_free, b.misc_use(name))
                for t in range(T):
                    ins = nc.tensor.transpose(misc_b[0:PARTS * NJ, t * P:(t + 1) * P],
                                              max_parts[:, g % 2, t, :, :].rearrange("p i j -> p (i j)"), id_b[:, :])
                ins.then_inc(misc_full, 1)

            def in_misc(b, name, columns, piece, bank=misc[:, :], free=None):
                what = name.rstrip("-")
                pieces, left = PIECES.get(what, 2), len(name) - len(what)
                if left == pieces - 1:
                    wait(pe, misc_free, b.misc_use(free) + 1 if free else b.misc_use(what))
                n = S // columns // pieces
                for t in range((pieces - 1 - left) * n, (pieces - left) * n):
                    ins = piece(t, bank[:, t * columns:(t + 1) * columns])
                if left == 0:
                    ins.then_inc(misc_full, 1)

            def turn(src):
                return lambda t, dst: nc.tensor.transpose(dst, src[:, t, :], id_f[:, :])

            def turn_att(i):
                def piece(t, dst):
                    tile, gp = 2 * i + t // 2, t % 2
                    return nc.tensor.transpose(dst, att_u[:, gp, tile * P:(tile + 1) * P], id_f[:, :])
                return piece

            def to_features(w, src):
                def piece(t, dst):
                    return nc.tensor.matmul(dst, w, src[:, t * S // 2:(t + 1) * S // 2], start=True, stop=True)
                return piece

            def to_tokens(src, w):
                return lambda t, dst: nc.tensor.matmul(dst, src[:, t * P:(t + 1) * P], w, start=True, stop=True)

            def second_product(t, dst):
                for c in range(FC):
                    i = D + FF + c * D
                    ins = nc.tensor.matmul(dst, hid[:, c, t * P:(t + 1) * P], w_post[:, i:i + D],
                                           start=(c == 0), stop=(c == FC - 1))
                return ins

            def item(b, name):
                u = b.u
                w_qkv = w_a if b.prep == "A" else w_in
                what, first = name.rstrip("-"), name[-1] == "-"
                if what == "off0":
                    turn_off(b, u + 1, 0, name)
                elif what in ("off1", "off2", "off3"):
                    turn_off(b, u, int(name[3]), name)
                elif what == "hT":
                    if first:
                        pe.wait_ge(norm_ready[0], u + 2)
                    in_misc(b, name, P, turn(x_n))
                elif what in ("q", "k"):
                    if b.prep == "B" and name == "q-":
                        pe.wait_ge(pb_in, (u + 2 - NA) * LOADS["pb"] * DMA)
                    i = 0 if what == "q" else D
                    in_misc(b, name, S // 2, to_features(w_qkv[:, i:i + D], h_T))
                elif what == "v":
                    in_misc(b, name, P, to_tokens(h_T, w_qkv[:, 2 * D:3 * D]))
                elif what in ("O0", "O1"):
                    if first:
                        pe.wait_ge(ev_done, 2 * u)
                    in_misc(b, name, P, turn_att(int(what[1])))
                elif what == "aT":
                    in_misc(b, name, P, turn(attn))
                elif what == "opA":
                    in_misc(b, name, P, to_tokens(attn_T, w_a[:, 3 * D:4 * D]))
                elif what == "opB":
                    if first:
                        pe.wait_ge(wp_in, (u - NA) * DMA)
                    in_misc(b, name, P, to_tokens(attn_T, w_post[:, 0:D]))
                elif what == "h2T":
                    if first:
                        pe.wait_ge(norm_ready[1], u)
                    in_misc(b, name, P, turn(h2_n))
                elif what == "gate":
                    pe.wait_ge(hsum_ready, u)
                    wait(pe, misc_free, b.misc_use(name))
                    nc.tensor.matmul(misc[:, 0:NE], h_sum_b[:, :], gw[:, :], start=True, stop=True).then_inc(misc_full, 1)
                elif what == "x1T":
                    if first:
                        pe.wait_ge(norm_ready[2], u - NA)
                    in_misc(b, name, P, turn(x1_n))
                elif what in ("ff0", "ff1", "ff2", "ff3"):
                    i = D + int(what[2]) * P
                    in_misc(b, name, S // 2, to_features(w_post[:, i:i + P], x1_T), hidden_bank(b, int(what[2])),
                            None if b.steps else "x1T")
                elif what == "out":
                    in_misc(b, name, P, second_product)

            walk(pe, slot_step, item, pv_step)

        @block.vector
        def _(dve):
            v = nc.vector

            chain = Chain(dve, setup_chain, 22, 0)
            dve.wait_ge(silu_exp, 1)
            chain.link(v.tensor_scalar(c_e[:, :], c_e[:, :], 1.0, None, ALU.add))
            chain.link(v.reciprocal(c_s[:, :], c_e[:, :]))
            v.tensor_tensor(c_s[:, :], c_s[:, :], c_T[:, :], ALU.mult).then_inc(silu_made, 1)
            dve.wait_ge(mod_mm, 1)
            chain.link(v.tensor_copy(mod_cols[:, :, :].rearrange("p m b -> p (m b)"), misc[:, 0:6 * NB]))
            v.tensor_scalar(mod_cols[:, 1:5:3, :], mod_cols[:, 1:5:3, :], 1.0, None, ALU.add).then_inc(cols_made, 1)

            def setup_rest():
                dve.wait_ge(mod_mm, 3)
                for i in range(2):
                    chain.link(v.tensor_copy(mod4[:, 3 * i:3 * i + 3, :].rearrange("b m d -> b (m d)"),
                                             s_ps[0:NB, i, 0:3 * D]))
                g_mod = mod4[:, 2:6:3, :]
                chain.link(v.tensor_scalar(mod_a[:, :, :], g_mod, -1.0, None, ALU.mult))
                chain.link(v.scalar_tensor_tensor(out=mod_a[:, :, :], in0=mod_a[:, :, :], scalar=0.25, in1=g_mod,
                                                  op0=ALU.max, op1=ALU.max))
                chain.link(v.tensor_scalar(mod_s[:, :, :], g_mod, 0.0, 2.0, ALU.is_ge, ALU.mult))
                chain.link(v.tensor_scalar(mod_s[:, :, :], mod_s[:, :, :], -1.0, None, ALU.add))
                v.tensor_tensor(g_mod, mod_s[:, :, :], mod_a[:, :, :], ALU.mult).then_inc(mod_made, 1)
                chain.link(v.memset(kstk[64:96, :, :], 1.0))
                chain.link(v.memset(vpad[:, :, :, :, :], 0.0))
                for g in range(NQ):
                    i = (g % 2) * VW + HD
                    chain.link(v.memset(vpad[:, :, g, :, i:i + 1], 1.0))
                for e in range(NE):
                    chain.link(v.memset(before[:, e, :], 0.0))
                    if e:
                        chain.link(v.memset(before[:, e, 0:e], 1.0))
                    ins = v.memset(e_no[:, e:e + 1], float(e))
                ins.then_inc(ones_made, 1)
                chain.end()

            def ln_stats(chain, i, src):
                for t in range(T):
                    ins = v.bn_stats(stats[:, i, t, :], src[:, t, :])
                chain.link(ins, bare_next=True)
                for t in range(T):
                    ins = v.bn_aggr(mv[:, i, t, :], stats[:, i, t, :])
                chain.link(ins)
                v.tensor_scalar(var_e[:, i, :], mv[:, i, :, 1], EPS, None, ALU.add).then_inc(var_ready[i], 1)

            def ln_end(chain, i, unit):
                dve.wait_ge(pow_ready[i], unit + 1)
                a, c = newton[:, i, 0, :], newton[:, i, 1, :]
                chain.link(v.tensor_tensor(a, rstd0[:, i, :], rstd0[:, i, :], ALU.mult))
                chain.link(v.tensor_tensor(c, a, var_e[:, i, :], ALU.mult))
                chain.link(v.tensor_scalar(a, c, -0.5, 1.5, ALU.mult, ALU.add))
                chain.link(v.tensor_tensor(rstd[:, i, :], a, rstd0[:, i, :], ALU.mult))
                chain.end()
                v.scalar_tensor_tensor(out=shift[:, i, :], in0=mv[:, i, :, 0], scalar=-1.0, in1=rstd[:, i, :],
                                       op0=ALU.mult, op1=ALU.mult).then_inc(rstd_ready[i], 1)

            def slot_step(b, tick, c):
                knd, unit = (b.steps, b.u) if tick < 8 else (b.prep, b.u + 1)
                if not knd:
                    return
                g = 2 + tick // T if tick < 8 else (tick - 8) // T
                t = tick % T
                keys = (t + 1) * P if knd == "A" else S
                n = b.u * NJ * TICKS + NJ * 8 + NJ * tick + c
                dve.wait_ge(s_full, n + 1)
                v.tensor_reduce(row_max[:, g % 2, t, c:c + 1], s_ps[:, (NJ * tick + c) % RING, 0:keys], AX.X, ALU.max)\
                 .then_inc(max_done, 1)

            def split_max(unit, g, n):
                q = g % 2
                dve.wait_ge(max_done, n)
                chain = Chain(dve, parts_chain, 3, unit * NQ + g)
                chain.link(v.tensor_scalar(max_parts[:, q, :, 0, :], row_max[:, q, :, :], -1.0, None, ALU.mult))
                chain.link(v.scalar_tensor_tensor(out=max_r[:, q, :, :], in0=row_max[:, q, :, :], scalar=-1.0,
                                                  in1=max_parts[:, q, :, 0, :], op0=ALU.mult, op1=ALU.subtract))
                chain.link(v.tensor_copy(max_parts[:, q, :, 1, :], max_r[:, q, :, :]))
                chain.end()
                v.tensor_tensor(max_parts[:, q, :, 2, :], max_r[:, q, :, :], max_parts[:, q, :, 1, :], ALU.subtract)\
                 .then_inc(parts_ready, 1)

            def pv_step(b, tick):
                pass

            open_chains = {}

            def item(b, name):
                u = b.u
                if name[0:2] == "mx":
                    g = int(name[2])
                    unit = u + 1 if g == 0 else u
                    split_max(unit, g, (unit * NQ + g + 1) * NJ * T)
                elif name == "ln1a":
                    n = u + 1
                    dve.wait_ge(pa_in, (n + 1) * LOADS["pa"] * DMA)
                    open_chains["ln1"] = Chain(dve, ln1_chain, 6, n)
                    ln_stats(open_chains["ln1"], 0, x_in)
                elif name == "ln1b":
                    ln_end(open_chains["ln1"], 0, u + 1)
                    if b.first < 0:
                        setup_rest()
                elif name in ("O0", "O1"):
                    i = int(name[1])
                    src = misc[:, :].rearrange("p (h c) -> p h c", c=VW)
                    dve.wait_ge(misc_full, b.misc_use(name) + 1)
                    v.reciprocal(recip[:, i, :], src[:, :, HD]).then_inc(rec_done, 1)
                    dve.wait_ge(rec_done, (u - 1) * 2 + i + 1)
                    v.tensor_tensor(attn[:, 2 * i:2 * i + 2, :].rearrange("p t (h d) -> p (t h) d", d=HD), src[:, :, 0:HD],
                                    recip[:, i, :].unsqueeze(2).to_broadcast([P, 2 * NQ * NJ, HD]), ALU.mult)\
                     .then_inc(misc_free, 1)
                elif name == "opA":
                    n = u - 1
                    dve.wait_ge(misc_full, b.misc_use(name) + 1)
                    dve.wait_ge(pre_ready["A"], n + 1)
                    wait(dve, a_out, n * LOADS["a_out"] * DMA)
                    v.tensor_tensor(t1[:, :, :], misc_t, over_tiles(mod_post[:, 0, :]), ALU.mult).then_inc(misc_free, 1)
                    dve.wait_ge(misc_free, b.misc_use(name) + 1)
                    v.tensor_tensor(x2[:, :, :], t1[:, :, :], x_pre[:, :, :], ALU.add).then_inc(x2_ready, 1)
                    wait(dve, x2_ready, n + 1, bare=True)
                elif name == "st2":
                    open_chains["ln2"] = Chain(dve, ln2_chain, 6, u - 1)
                    ln_stats(open_chains["ln2"], 1, x2)
                elif name == "ln2":
                    ln_end(open_chains["ln2"], 1, u - 1)
                elif name == "gsum":
                    dve.wait_ge(misc_free, b.misc_use("h2T") + 1)
                    v.tensor_copy(h_sum_b[:, :], h_sum[:, :].to_broadcast([P, P])).then_inc(hsum_ready, 1)
                elif name == "gate":
                    n = u - 1
                    dve.wait_ge(misc_full, b.misc_use(name) + 1)
                    v.scalar_tensor_tensor(out=lg[:, :], in0=misc[:, 0:NE], scalar=1.0 / S, in1=gb_b[:, :],
                                           op0=ALU.mult, op1=ALU.add).then_inc(misc_free, 1)
                    dve.wait_ge(misc_free, b.misc_use(name) + 1)
                    c = Chain(dve, gate_chain, 11, n)
                    c.link(v.tensor_reduce(lmax[:, :], lg[:, :], AX.X, ALU.max))
                    v.tensor_scalar(lsh[:, :], lg[:, :], lmax[:, 0:1], None, ALU.subtract).then_inc(lsh_ready, 1)
                    other = lg[:, :].unsqueeze(1).to_broadcast([P, NE, NE])
                    own = lg[:, :].unsqueeze(2).to_broadcast([P, NE, NE])
                    v.tensor_tensor(gt[:, :, :], other, own, ALU.is_gt)
                    c.link(v.tensor_tensor(eq[:, :, :], other, own, ALU.is_equal))
                    c.link(v.tensor_tensor(eq[:, :, :], eq[:, :, :], before[:, :, :], ALU.mult))
                    c.link(v.tensor_tensor(gt[:, :, :], gt[:, :, :], eq[:, :, :], ALU.add))
                    c.link(v.tensor_reduce(rank[:, :], gt[:, :, :], AX.X, ALU.add))
                    for k in range(TOPK):
                        ins = v.tensor_scalar(pick[:, k, :], rank[:, :], float(k), None, ALU.is_equal)
                    c.link(ins)
                    c.link(v.tensor_tensor(pick_n[:, :, :], pick[:, :, :],
                                           e_no[:, :].unsqueeze(1).to_broadcast([P, TOPK, NE]), ALU.mult))
                    c.link(v.tensor_reduce(nsel_f[:, :], pick_n[:, :, :], AX.X, ALU.add))
                    v.tensor_copy(nsel[:, bass.ds(n * TOPK, TOPK)], nsel_f[:, :])
                    dve.wait_ge(lexp_ready, n + 1)
                    c.link(v.tensor_reduce(lsum[:, :], lexp[:, :], AX.X, ALU.add))
                    c.link(v.reciprocal(lrec[:, :], lsum[:, :]))
                    c.link(v.scalar_tensor_tensor(out=pick_w[:, :, :], in0=pick[:, :, :], scalar=lrec[:, 0:1],
                                                  in1=lexp[:, :].unsqueeze(1).to_broadcast([P, TOPK, NE]),
                                                  op0=ALU.mult, op1=ALU.mult))
                    c.end()
                    v.tensor_reduce(wsel[:, bass.ds(n * TOPK, TOPK)], pick_w[:, :, :], AX.X, ALU.add)\
                     .then_inc(sel_ready, 1)
                elif name in ("opB", "out"):
                    n = u - 1 - NA
                    dve.wait_ge(misc_full, b.misc_use(name) + 1)
                    if name == "opB":
                        plus = x_pre
                        dve.wait_ge(pre_ready["B"], n + 1)
                    else:
                        plus = x1
                        dve.wait_ge(x1_ready, n + 1)
                    v.tensor_tensor(t2[:, :, :], misc_t, plus[:, :, :], ALU.add).then_inc(misc_free, 1)
                    wait(dve, misc_free, b.misc_use(name) + 1, bare=True)
                elif name in ("st3", "st4"):
                    open_chains[name] = Chain(dve, ln3_chain if name == "st3" else ln4_chain, 6, u - 1 - NA)
                    ln_stats(open_chains[name], 2 if name == "st3" else 3, t2)
                elif name in ("ln3", "ln4"):
                    ln_end(open_chains["st" + name[2]], 2 if name == "ln3" else 3, u - 1 - NA)

            walk(dve, slot_step, item, pv_step)


def kernel(**inputs):
    import numpy as _np
    import concourse.bacc as _bacc
    from concourse import mybir as _mybir
    from concourse.bass_utils import run_bass_kernel_spmd as _run

    a = {k: _np.asarray(v) for k, v in inputs.items()}
    at = {k[len("L0_attn_"):]: v for k, v in a.items() if k.startswith("L0_attn_")}
    ff = {k[len("L0_ffn_"):]: v for k, v in a.items() if k.startswith("L0_ffn_")}
    ne = ff["gate_w"].shape[0]
    turned = lambda w: w.transpose(0, 2, 1)
    lin2 = turned(ff["lin2_w"]).reshape(ne, FC, P, D).transpose(0, 2, 1, 3).reshape(ne, P, FC * D)
    cat = _np.concatenate
    arrays = {
        "x": at["x"],
        "w_attn": cat([at["Wq"], at["Wk"], at["Wv"], at["Wmix"]], axis=1),
        "cols_attn": _np.stack([at["bq"], at["bk"], at["bv"]], axis=1),
        "row_attn": at["bmix"],
        "w_exp": cat([turned(ff["in_proj_w"]), turned(ff["in_proj_b"][:, 0:2 * D].reshape(ne, 2, D)),
                      turned(ff["out_proj_w"]), turned(ff["lin1_w"]), lin2,
                      turned(ff["lin1_b"].reshape(ne, FC, P)),
                      turned(_np.stack([ff["in_proj_b"][:, 2 * D:3 * D], ff["ln1_w"], ff["ln1_b"]], axis=1))], axis=2),
        "rows_exp": cat([ff["out_proj_b"], ff["ln1_w"], ff["ln1_b"], ff["lin2_b"],
                         ff["ln2_w"], ff["ln2_b"]], axis=1),
        "gate_wT": ff["gate_w"].T,
        "gate_b": ff["gate_b"],
        "cT": a["L0_c"].T,
        "wmod": a["L0_wmod"],
    }
    arrays = {f"in_{k}": _np.ascontiguousarray(v) for k, v in arrays.items()}
    nc = _bacc.Bacc("TRN2", target_bir_lowering=False, num_devices=1)
    args = [nc.dram_tensor(k, v.shape, _mybir.dt.from_np(v.dtype), kind="ExternalInput").ap() for k, v in arrays.items()]
    args.append(nc.dram_tensor("out_x", arrays["in_x"].shape, _mybir.dt.float32, kind="ExternalOutput").ap())
    adaln_kernel(nc, *args)
    r = _run(nc, [arrays], core_ids=[0])
    return r.results[0]["out_x"]
```
